# Optimizing a Trainium2 kernel written in Bass

```python
import numpy as np
import jax
import jax.numpy as jnp

def _softmax(x, axis=-1):
    return jax.nn.softmax(x, axis=axis)

def _gelu(x):
    return jax.nn.gelu(x, approximate=True)

def _silu(x):
    return jax.nn.silu(x)

def _sigmoid(x):
    return jax.nn.sigmoid(x)

def _layernorm(x, axis=-1, eps=1e-05):
    m = jnp.mean(x, axis=axis, keepdims=True)
    v = jnp.var(x, axis=axis, keepdims=True)
    return (x - m) / jnp.sqrt(v + eps)

def _scatter_add(tgt, idx, src, axis=0):
    return tgt.at[idx].add(src)

def _segment_sum(src, seg, n):
    return jax.ops.segment_sum(src, seg, n)
kernel_name = 'mk_lm_tower_d4_tok_ids1024_r4_250429'

def setup_inputs(seed: int=0):
    np.random.seed(seed)
    _w = jnp.asarray

    def _rec_inputs():
        import jax
        import jax.numpy as jnp
        _rk = jax.random.key(seed)
        x = jax.random.randint(jax.random.fold_in(_rk, 1), (8, 512), 0, 25, jnp.int32)
        itok_BS_1_7 = jax.random.randint(jax.random.fold_in(_rk, 21), (8, 512), 1, 8, jnp.int32)
        itok_BS_0_1439 = jax.random.randint(jax.random.fold_in(_rk, 22), (8, 512), 0, 360, jnp.int32)
        return (x, itok_BS_1_7, itok_BS_0_1439)
    x, itok_BS_1_7, itok_BS_0_1439 = _rec_inputs()

    def _L0_tok_setup():
        import jax, jax.numpy as jnp
        import numpy as np
        import math
        LN_EPS = 1e-05
        TWO_PI = 2.0 * math.pi

        def _ln(x, g, b):
            m = jnp.mean(x, axis=-1, keepdims=True)
            v = jnp.mean((x - m) ** 2, axis=-1, keepdims=True)
            return (x - m) * jax.lax.rsqrt(v + LN_EPS) * g + b

        def _encoder(feat, w1, b1, g, be, w2, b2):
            h = _ln(feat @ w1 + b1, g, be)
            return jax.nn.gelu(h, approximate=False) @ w2 + b2
        key = jax.random.key(seed)
        ks = jax.random.split(key, 12)
        B, S, D, DT = (64, 512, 256, 64)
        s = 0.02
        hour_tab = (jax.random.normal(ks[0], (25, DT)) * s).at[0].set(0.0)
        wd_tab = (jax.random.normal(ks[1], (8, DT)) * s).at[0].set(0.0)
        return {'hours': jax.random.randint(ks[2], (B, S), 1, 25), 'weekdays': jax.random.randint(ks[3], (B, S), 1, 8), 'start_mins': jax.random.randint(ks[4], (B, S), 0, 360), 'hour_tab': hour_tab, 'wd_tab': wd_tab, 't_w1': jax.random.normal(ks[5], (2, DT)) * s, 't_b1': jnp.zeros((DT,)), 't_gamma': jnp.ones((DT,)), 't_beta': jnp.zeros((DT,)), 't_w2': jax.random.normal(ks[6], (DT, DT)) * s, 't_b2': jnp.zeros((DT,)), 'd_w1': jax.random.normal(ks[7], (2, DT)) * s, 'd_b1': jnp.zeros((DT,)), 'd_gamma': jnp.ones((DT,)), 'd_beta': jnp.zeros((DT,)), 'd_w2': jax.random.normal(ks[8], (DT, DT)) * s, 'd_b2': jnp.zeros((DT,)), 'proj_w': jax.random.normal(ks[9], (4 * DT, D)) * s, 'proj_b': jnp.zeros((D,))}
    _L0_tok_all = _L0_tok_setup()
    _L0_tok_in = {k: v for k, v in _L0_tok_all.items() if k in ('hour_tab', 'wd_tab', 't_w1', 't_b1', 't_gamma', 't_beta', 't_w2', 't_b2', 'd_w1', 'd_b1', 'd_gamma', 'd_beta', 'd_w2', 'd_b2', 'proj_w', 'proj_b')}
    del _L0_tok_all

    def _L0_attn_setup():
        import jax, jax.numpy as jnp
        import numpy as np
        N_HEADS = 16
        HIDDEN = 256
        HEAD_DIM = 64
        BSZ = 4
        SEQ = 256
        SCALE = HEAD_DIM ** (-0.5)
        key = jax.random.key(seed)
        k_x, k_q, k_k, k_v, k_o = jax.random.split(key, 5)
        s = HIDDEN ** (-0.5)
        return {'x': jax.random.normal(k_x, (BSZ, SEQ, HIDDEN), dtype=jnp.float32), 'wq': jax.random.normal(k_q, (N_HEADS * HEAD_DIM, HIDDEN), dtype=jnp.float32) * s, 'wk': jax.random.normal(k_k, (N_HEADS * HEAD_DIM, HIDDEN), dtype=jnp.float32) * s, 'wv': jax.random.normal(k_v, (N_HEADS * HEAD_DIM, HIDDEN), dtype=jnp.float32) * s, 'wo': jax.random.normal(k_o, (HIDDEN, N_HEADS * HEAD_DIM), dtype=jnp.float32) * s}
    _L0_attn_all = _L0_attn_setup()
    _L0_attn_in = {k: v for k, v in _L0_attn_all.items() if k in ('wq', 'wk', 'wv', 'wo')}
    del _L0_attn_all

    def _L0_ffn_setup():
        import jax, jax.numpy as jnp
        import numpy as np
        D_MODEL, D_FF, D2, DL = (256, 1024, 64, 64)
        D1 = D_FF // D2
        BATCH, SEQ = (2, 256)
        KERNEL_SCALE = D2 ** 0.5
        key = jax.random.key(seed)
        ks = jax.random.split(key, 7)
        xav = lambda k, shape, fan: jax.random.normal(k, shape, jnp.float32) * (2.0 / sum(fan)) ** 0.5
        x = jax.random.normal(ks[0], (BATCH, SEQ, D_MODEL), jnp.float32)
        m1 = xav(ks[1], (D_MODEL, DL), (D_MODEL, DL))
        m2 = xav(ks[2], (DL, D1, D2), (DL, D_FF))
        mb = jax.random.normal(ks[3], (D1, D2), jnp.float32)
        w1 = xav(ks[4], (D_MODEL, D1, D2), (D_MODEL, D_FF))
        w2 = xav(ks[5], (D2, D1, D_MODEL), (D_FF, D_MODEL)) * KERNEL_SCALE
        b2 = jax.random.normal(ks[6], (D_MODEL,), jnp.float32)
        return {'x': x, 'm1': m1, 'm2': m2, 'mb': mb, 'w1': w1, 'w2': w2, 'b2': b2}
    _L0_ffn_all = _L0_ffn_setup()
    _L0_ffn_in = {k: v for k, v in _L0_ffn_all.items() if k in ('m1', 'm2', 'mb', 'w1', 'w2', 'b2')}
    del _L0_ffn_all

    def _L1_attn_setup():
        import jax, jax.numpy as jnp
        import numpy as np
        B, T, D = (4, 512, 256)
        H, DK, DV = (8, 128, 128)

        def _l2norm(u, eps=1e-12):
            n = jnp.sqrt(jnp.sum(u * u, axis=-1, keepdims=True))
            return u / jnp.maximum(n, eps)
        key = jax.random.key(seed)
        ks = jax.random.split(key, 6)
        s = 0.02
        x = jax.random.normal(ks[0], (B, T, D), dtype=jnp.float32)
        Wq = jax.random.normal(ks[1], (D, H * DK), dtype=jnp.float32) * s
        Wk = jax.random.normal(ks[2], (D, H * DK), dtype=jnp.float32) * s
        Wv = jax.random.normal(ks[3], (D, H * DV), dtype=jnp.float32) * s
        Wg = jax.random.normal(ks[4], (D, H * DK), dtype=jnp.float32) * s
        Wo = jax.random.normal(ks[5], (H * DV, D), dtype=jnp.float32) * s
        return {'x': x, 'Wq': Wq, 'Wk': Wk, 'Wv': Wv, 'Wg': Wg, 'Wo': Wo}
    _L1_attn_all = _L1_attn_setup()
    _L1_attn_in = {k: v for k, v in _L1_attn_all.items() if k in ('Wq', 'Wk', 'Wv', 'Wg', 'Wo')}
    del _L1_attn_all

    def _L1_ffn_setup():
        import jax, jax.numpy as jnp
        import numpy as np
        D_MODEL = 256
        M = 64
        INNER = 16
        key = jax.random.key(seed)
        ks = jax.random.split(key, 9)

        def init(k, shape, fan_in):
            bound = 1.0 / np.sqrt(fan_in)
            return jax.random.uniform(k, shape, jnp.float32, -bound, bound)
        x = jax.random.normal(ks[0], (16, 1024, D_MODEL), dtype=jnp.float32)
        Win = init(ks[1], (D_MODEL, M), D_MODEL)
        bin_ = init(ks[2], (M,), D_MODEL)
        W1 = init(ks[3], (M, INNER), 1)
        b1 = init(ks[4], (M, INNER), 1)
        W2 = init(ks[5], (M, INNER), INNER)
        b2 = init(ks[6], (M,), INNER)
        Wout = init(ks[7], (M, D_MODEL), M)
        bout = init(ks[8], (D_MODEL,), M)
        return {'x': x, 'Win': Win, 'bin_': bin_, 'W1': W1, 'b1': b1, 'W2': W2, 'b2': b2, 'Wout': Wout, 'bout': bout}
    _L1_ffn_all = _L1_ffn_setup()
    _L1_ffn_in = {k: v for k, v in _L1_ffn_all.items() if k in ('Win', 'bin_', 'W1', 'b1', 'W2', 'b2', 'Wout', 'bout')}
    del _L1_ffn_all

    def _L2_attn_setup():
        import jax, jax.numpy as jnp
        import numpy as np
        import math
        NUM_HEADS = 16
        D_MODEL = 256
        B, T = (1, 1024)
        key = jax.random.key(seed)
        kx, kq, kk, kv, ko = jax.random.split(key, 5)
        s = 1.0 / math.sqrt(D_MODEL)
        return {'x': jax.random.normal(kx, (B, T, D_MODEL), dtype=jnp.float32), 'Wq': jax.random.normal(kq, (D_MODEL, D_MODEL), dtype=jnp.float32) * s, 'Wk': jax.random.normal(kk, (D_MODEL, D_MODEL), dtype=jnp.float32) * s, 'Wv': jax.random.normal(kv, (D_MODEL, D_MODEL), dtype=jnp.float32) * s, 'Wo': jax.random.normal(ko, (D_MODEL, D_MODEL), dtype=jnp.float32) * s}
    _L2_attn_all = _L2_attn_setup()
    _L2_attn_in = {k: v for k, v in _L2_attn_all.items() if k in ('Wq', 'Wk', 'Wv', 'Wo')}
    del _L2_attn_all

    def _L2_ffn_setup():
        import jax, jax.numpy as jnp
        import numpy as np
        E = 8
        TOP_K = 2
        CAP_FACTOR = 1.25
        MIN_CAP = 4
        SCORE_SCALE = 1.0

        def _ffn(x, w1, b1, w2, b2):
            return jax.nn.gelu(x @ w1 + b1, approximate=False) @ w2 + b2
        key = jax.random.key(seed)
        ks = jax.random.split(key, 6)
        B, S, D, I = (4, 512, 256, 1024)
        std = 0.02
        return {'x': jax.random.normal(ks[0], (B, S, D), jnp.float32), 'Wr': jax.random.normal(ks[1], (E, D), jnp.float32) * std, 'W1': jax.random.normal(ks[2], (E, D, I), jnp.float32) * std, 'b1': jnp.zeros((E, I), jnp.float32), 'W2': jax.random.normal(ks[3], (E, I, D), jnp.float32) * std, 'b2': jnp.zeros((E, D), jnp.float32), 'fw1': jax.random.normal(ks[4], (D, I), jnp.float32) * std, 'fb1': jnp.zeros((I,), jnp.float32), 'fw2': jax.random.normal(ks[5], (I, D), jnp.float32) * std, 'fb2': jnp.zeros((D,), jnp.float32)}
    _L2_ffn_all = _L2_ffn_setup()
    _L2_ffn_in = {k: v for k, v in _L2_ffn_all.items() if k in ('Wr', 'W1', 'b1', 'W2', 'b2', 'fw1', 'fb1', 'fw2', 'fb2')}
    del _L2_ffn_all

    def _L3_attn_setup():
        import jax, jax.numpy as jnp
        import numpy as np
        EMBED_DIM = 256
        N_HEADS = 16
        HEAD_DIM = EMBED_DIM // N_HEADS
        N_FEATURES = 64
        EPS = 0.0001

        def softmax_kernel(data, projection_matrix, eps=EPS):
            data_normalizer = data.shape[-1] ** (-0.25)
            proj = jnp.einsum('bhnd,fd->bhnf', data, projection_matrix) * data_normalizer
            proj_max = jnp.max(proj, axis=-1, keepdims=True)
            return jnp.exp(proj - proj_max + eps)
        key = jax.random.key(seed)
        k_x, k_w1, k_b1, k_w2, k_b2, k_p = jax.random.split(key, 6)
        B, N, D = (4, 1024, EMBED_DIM)
        s1 = 1.0 / np.sqrt(D)
        x = jax.random.normal(k_x, (B, N, D), dtype=jnp.float32)
        W_qkv = jax.random.uniform(k_w1, (3 * D, D), dtype=jnp.float32, minval=-s1, maxval=s1)
        b_qkv = jax.random.uniform(k_b1, (3 * D,), dtype=jnp.float32, minval=-s1, maxval=s1)
        W_proj = jax.random.uniform(k_w2, (D, D), dtype=jnp.float32, minval=-s1, maxval=s1)
        b_proj = jax.random.uniform(k_b2, (D,), dtype=jnp.float32, minval=-s1, maxval=s1)
        pm = jax.random.normal(k_p, (N_FEATURES, HEAD_DIM), dtype=jnp.float32)
        pm = pm / jnp.linalg.norm(pm, axis=-1, keepdims=True)
        return {'x': x, 'W_qkv': W_qkv, 'b_qkv': b_qkv, 'W_proj': W_proj, 'b_proj': b_proj, 'proj_mat': pm}
    _L3_attn_all = _L3_attn_setup()
    _L3_attn_in = {k: v for k, v in _L3_attn_all.items() if k in ('W_qkv', 'b_qkv', 'W_proj', 'b_proj', 'proj_mat')}
    del _L3_attn_all

    def _L3_ffn_setup():
        import jax, jax.numpy as jnp
        import numpy as np
        D_MODEL = 256
        EXPANSION = 4
        D_HIDDEN = D_MODEL * EXPANSION
        NUM_STAGES = int(np.log2(D_HIDDEN))

        def butterfly(y, weights, dim):
            lead = y.shape[:-1]
            for stage in range(weights.shape[0]):
                s = 2 ** stage
                nb = dim // (2 * s)
                yr = y.reshape(*lead, nb, 2, s)
                a = yr[..., 0, :]
                b = yr[..., 1, :]
                w = weights[stage].reshape(nb, s, 2, 2)
                na = w[..., 0, 0] * a + w[..., 0, 1] * b
                nb2 = w[..., 1, 0] * a + w[..., 1, 1] * b
                y = jnp.stack([na, nb2], axis=-2).reshape(*lead, dim)
            return y
        key = jax.random.key(seed)
        ks = jax.random.split(key, 6)
        B, S = (4, 512)
        x = jax.random.normal(ks[0], (B, S, D_MODEL), jnp.float32)
        W_exp = jax.random.normal(ks[1], (D_MODEL, D_HIDDEN), jnp.float32) * 0.02
        b_exp = jnp.zeros((D_HIDDEN,), jnp.float32)
        up_weights = jax.random.normal(ks[2], (NUM_STAGES, D_HIDDEN // 2, 2, 2), jnp.float32) * 0.02
        up_bias = jnp.zeros((D_HIDDEN,), jnp.float32)
        down_weights = jax.random.normal(ks[3], (NUM_STAGES, D_HIDDEN // 2, 2, 2), jnp.float32) * 0.02
        W_con = jax.random.normal(ks[4], (D_HIDDEN, D_MODEL), jnp.float32) * 0.02
        b_con = jnp.zeros((D_MODEL,), jnp.float32)
        down_bias = jnp.zeros((D_MODEL,), jnp.float32)
        return dict(x=x, W_exp=W_exp, b_exp=b_exp, up_weights=up_weights, up_bias=up_bias, down_weights=down_weights, W_con=W_con, b_con=b_con, down_bias=down_bias)
    _L3_ffn_all = _L3_ffn_setup()
    _L3_ffn_in = {k: v for k, v in _L3_ffn_all.items() if k in ('W_exp', 'b_exp', 'up_weights', 'up_bias', 'down_weights', 'W_con', 'b_con', 'down_bias')}
    del _L3_ffn_all
    return {'x': x, 'itok_BS_1_7': itok_BS_1_7, 'itok_BS_0_1439': itok_BS_0_1439, 'L0_tok_hour_tab': _L0_tok_in['hour_tab'], 'L0_tok_wd_tab': _L0_tok_in['wd_tab'], 'L0_tok_t_w1': _L0_tok_in['t_w1'], 'L0_tok_t_b1': _L0_tok_in['t_b1'], 'L0_tok_t_gamma': _L0_tok_in['t_gamma'], 'L0_tok_t_beta': _L0_tok_in['t_beta'], 'L0_tok_t_w2': _L0_tok_in['t_w2'], 'L0_tok_t_b2': _L0_tok_in['t_b2'], 'L0_tok_d_w1': _L0_tok_in['d_w1'], 'L0_tok_d_b1': _L0_tok_in['d_b1'], 'L0_tok_d_gamma': _L0_tok_in['d_gamma'], 'L0_tok_d_beta': _L0_tok_in['d_beta'], 'L0_tok_d_w2': _L0_tok_in['d_w2'], 'L0_tok_d_b2': _L0_tok_in['d_b2'], 'L0_tok_proj_w': _L0_tok_in['proj_w'], 'L0_tok_proj_b': _L0_tok_in['proj_b'], 'L0_attn_wq': _L0_attn_in['wq'], 'L0_attn_wk': _L0_attn_in['wk'], 'L0_attn_wv': _L0_attn_in['wv'], 'L0_attn_wo': _L0_attn_in['wo'], 'L0_ffn_m1': _L0_ffn_in['m1'], 'L0_ffn_m2': _L0_ffn_in['m2'], 'L0_ffn_mb': _L0_ffn_in['mb'], 'L0_ffn_w1': _L0_ffn_in['w1'], 'L0_ffn_w2': _L0_ffn_in['w2'], 'L0_ffn_b2': _L0_ffn_in['b2'], 'L1_attn_Wq': _L1_attn_in['Wq'], 'L1_attn_Wk': _L1_attn_in['Wk'], 'L1_attn_Wv': _L1_attn_in['Wv'], 'L1_attn_Wg': _L1_attn_in['Wg'], 'L1_attn_Wo': _L1_attn_in['Wo'], 'L1_ffn_Win': _L1_ffn_in['Win'], 'L1_ffn_bin_': _L1_ffn_in['bin_'], 'L1_ffn_W1': _L1_ffn_in['W1'], 'L1_ffn_b1': _L1_ffn_in['b1'], 'L1_ffn_W2': _L1_ffn_in['W2'], 'L1_ffn_b2': _L1_ffn_in['b2'], 'L1_ffn_Wout': _L1_ffn_in['Wout'], 'L1_ffn_bout': _L1_ffn_in['bout'], 'L2_attn_Wq': _L2_attn_in['Wq'], 'L2_attn_Wk': _L2_attn_in['Wk'], 'L2_attn_Wv': _L2_attn_in['Wv'], 'L2_attn_Wo': _L2_attn_in['Wo'], 'L2_ffn_Wr': _L2_ffn_in['Wr'], 'L2_ffn_W1': _L2_ffn_in['W1'], 'L2_ffn_b1': _L2_ffn_in['b1'], 'L2_ffn_W2': _L2_ffn_in['W2'], 'L2_ffn_b2': _L2_ffn_in['b2'], 'L2_ffn_fw1': _L2_ffn_in['fw1'], 'L2_ffn_fb1': _L2_ffn_in['fb1'], 'L2_ffn_fw2': _L2_ffn_in['fw2'], 'L2_ffn_fb2': _L2_ffn_in['fb2'], 'L3_attn_W_qkv': _L3_attn_in['W_qkv'], 'L3_attn_b_qkv': _L3_attn_in['b_qkv'], 'L3_attn_W_proj': _L3_attn_in['W_proj'], 'L3_attn_b_proj': _L3_attn_in['b_proj'], 'L3_attn_proj_mat': _L3_attn_in['proj_mat'], 'L3_ffn_W_exp': _L3_ffn_in['W_exp'], 'L3_ffn_b_exp': _L3_ffn_in['b_exp'], 'L3_ffn_up_weights': _L3_ffn_in['up_weights'], 'L3_ffn_up_bias': _L3_ffn_in['up_bias'], 'L3_ffn_down_weights': _L3_ffn_in['down_weights'], 'L3_ffn_W_con': _L3_ffn_in['W_con'], 'L3_ffn_b_con': _L3_ffn_in['b_con'], 'L3_ffn_down_bias': _L3_ffn_in['down_bias']}

def reference(x, itok_BS_1_7, itok_BS_0_1439, L0_tok_hour_tab, L0_tok_wd_tab, L0_tok_t_w1, L0_tok_t_b1, L0_tok_t_gamma, L0_tok_t_beta, L0_tok_t_w2, L0_tok_t_b2, L0_tok_d_w1, L0_tok_d_b1, L0_tok_d_gamma, L0_tok_d_beta, L0_tok_d_w2, L0_tok_d_b2, L0_tok_proj_w, L0_tok_proj_b, L0_attn_wq, L0_attn_wk, L0_attn_wv, L0_attn_wo, L0_ffn_m1, L0_ffn_m2, L0_ffn_mb, L0_ffn_w1, L0_ffn_w2, L0_ffn_b2, L1_attn_Wq, L1_attn_Wk, L1_attn_Wv, L1_attn_Wg, L1_attn_Wo, L1_ffn_Win, L1_ffn_bin_, L1_ffn_W1, L1_ffn_b1, L1_ffn_W2, L1_ffn_b2, L1_ffn_Wout, L1_ffn_bout, L2_attn_Wq, L2_attn_Wk, L2_attn_Wv, L2_attn_Wo, L2_ffn_Wr, L2_ffn_W1, L2_ffn_b1, L2_ffn_W2, L2_ffn_b2, L2_ffn_fw1, L2_ffn_fb1, L2_ffn_fw2, L2_ffn_fb2, L3_attn_W_qkv, L3_attn_b_qkv, L3_attn_W_proj, L3_attn_b_proj, L3_attn_proj_mat, L3_ffn_W_exp, L3_ffn_b_exp, L3_ffn_up_weights, L3_ffn_up_bias, L3_ffn_down_weights, L3_ffn_W_con, L3_ffn_b_con, L3_ffn_down_bias):
    import jax
    import jax.numpy as jnp

    def _L0_tok_ref(hours, weekdays, start_mins, hour_tab, wd_tab, t_w1, t_b1, t_gamma, t_beta, t_w2, t_b2, d_w1, d_b1, d_gamma, d_beta, d_w2, d_b2, proj_w, proj_b):
        import jax, jax.numpy as jnp
        import numpy as np
        import math
        LN_EPS = 1e-05
        TWO_PI = 2.0 * math.pi

        def _ln(x, g, b):
            m = jnp.mean(x, axis=-1, keepdims=True)
            v = jnp.mean((x - m) ** 2, axis=-1, keepdims=True)
            return (x - m) * jax.lax.rsqrt(v + LN_EPS) * g + b

        def _encoder(feat, w1, b1, g, be, w2, b2):
            h = _ln(feat @ w1 + b1, g, be)
            return jax.nn.gelu(h, approximate=False) @ w2 + b2
        hour_emb = hour_tab[hours]
        weekday_emb = wd_tab[weekdays]
        hour_angle = start_mins.astype(jnp.float32) * (TWO_PI / 1440.0)
        hour_feat = jnp.stack([jnp.sin(hour_angle), jnp.cos(hour_angle)], axis=-1)
        day_angle = weekdays.astype(jnp.float32) * (TWO_PI / 7.0)
        day_feat = jnp.stack([jnp.sin(day_angle), jnp.cos(day_angle)], axis=-1)
        time_enc = _encoder(hour_feat, t_w1, t_b1, t_gamma, t_beta, t_w2, t_b2)
        day_enc = _encoder(day_feat, d_w1, d_b1, d_gamma, d_beta, d_w2, d_b2)
        combined = jnp.concatenate([hour_emb, weekday_emb, time_enc, day_enc], axis=-1)
        return combined @ proj_w + proj_b

    def _L0_attn_ref(x, wq, wk, wv, wo):
        import jax, jax.numpy as jnp
        import numpy as np
        N_HEADS = 16
        HIDDEN = 256
        HEAD_DIM = 64
        BSZ = 4
        SEQ = 256
        SCALE = HEAD_DIM ** (-0.5)
        bsz, seqlen, _ = x.shape
        xq = jnp.einsum('bsh,oh->bso', x, wq)
        xk = jnp.einsum('bsh,oh->bso', x, wk)
        xv = jnp.einsum('bsh,oh->bso', x, wv)
        xq = xq.reshape(bsz, N_HEADS, seqlen, HEAD_DIM)
        xk = xk.reshape(bsz, N_HEADS, seqlen, HEAD_DIM)
        xv = xv.reshape(bsz, N_HEADS, seqlen, HEAD_DIM)
        scores = jnp.einsum('bhid,bhjd->bhij', xq, xk) * SCALE
        scores = jax.nn.softmax(scores, axis=-1)
        out = jnp.einsum('bhij,bhjd->bhid', scores, xv)
        out = out.reshape(bsz, seqlen, N_HEADS * HEAD_DIM)
        return jnp.einsum('bso,ho->bsh', out, wo)

    def _L0_ffn_ref(x, m1, m2, mb, w1, w2, b2):
        import jax, jax.numpy as jnp
        import numpy as np
        D_MODEL, D_FF, D2, DL = (256, 1024, 64, 64)
        D1 = D_FF // D2
        BATCH, SEQ = (2, 256)
        KERNEL_SCALE = D2 ** 0.5
        x_shape = x.shape
        xf = x.reshape(-1, x_shape[-1])
        d1 = w1.shape[1]
        lr = xf @ m1
        mask_logits = jnp.einsum('bl,lxy->bxy', lr, m2) + mb
        quant_mask = jnp.argmax(mask_logits, axis=-1)
        w1p = jnp.transpose(w1, (1, 2, 0))
        w2p = jnp.transpose(w2, (1, 0, 2))
        j = jnp.arange(d1)[None, :]
        w = w1p[j, quant_mask]
        mid = jnp.einsum('ai,aji->aj', xf, w)
        relu = jax.nn.relu(mid)
        v = w2p[j, quant_mask]
        res = jnp.einsum('ai,aij->aj', relu, v) + b2
        return res.reshape(x_shape)

    def _L1_attn_ref(x, Wq, Wk, Wv, Wg, Wo):
        import jax, jax.numpy as jnp
        import numpy as np
        B, T, D = (4, 512, 256)
        H, DK, DV = (8, 128, 128)

        def _l2norm(u, eps=1e-12):
            n = jnp.sqrt(jnp.sum(u * u, axis=-1, keepdims=True))
            return u / jnp.maximum(n, eps)
        Bb, Tt, _ = x.shape
        q = _l2norm((x @ Wq).reshape(Bb, Tt, H, DK))
        k = _l2norm((x @ Wk).reshape(Bb, Tt, H, DK))
        v = (x @ Wv).reshape(Bb, Tt, H, DV)
        alpha = jax.nn.sigmoid(x @ Wg).reshape(Bb, Tt, H, DK)

        def step(S, qkva):
            q_t, k_t, v_t, a_t = qkva
            S = a_t[..., None] * S + k_t[..., None] * v_t[:, :, None, :]
            o_t = jnp.einsum('bhkv,bhk->bhv', S, q_t)
            return (S, o_t)
        S0 = jnp.zeros((Bb, H, DK, DV), dtype=x.dtype)
        xs = (q.swapaxes(0, 1), k.swapaxes(0, 1), v.swapaxes(0, 1), alpha.swapaxes(0, 1))
        _, o = jax.lax.scan(step, S0, xs)
        o = o.swapaxes(0, 1).reshape(Bb, Tt, H * DV)
        return o @ Wo

    def _L1_ffn_ref(x, Win, bin_, W1, b1, W2, b2, Wout, bout):
        import jax, jax.numpy as jnp
        import numpy as np
        D_MODEL = 256
        M = 64
        INNER = 16
        s = jnp.einsum('btd,dm->btm', x, Win) + bin_
        h = jax.nn.relu(s[..., None] * W1 + b1)
        g = jnp.einsum('btmh,mh->btm', h, W2) + b2
        out = jnp.einsum('btm,md->btd', g, Wout) + bout
        return out

    def _L2_attn_ref(x, Wq, Wk, Wv, Wo):
        import jax, jax.numpy as jnp
        import numpy as np
        import math
        NUM_HEADS = 16
        D_MODEL = 256
        B, T = (1, 1024)
        Bx, Tx, D = x.shape
        H = NUM_HEADS
        dk = D // H
        q = (x @ Wq.T).reshape(Bx, Tx, H, dk)
        k = (x @ Wk.T).reshape(Bx, Tx, H, dk)
        v = (x @ Wv.T).reshape(Bx, Tx, H, dk)
        scores = jnp.einsum('bthd,bshd->bhts', q, k) / math.sqrt(dk)
        causal_mask = jnp.triu(jnp.ones((Tx, Tx), dtype=bool), k=1)
        scores = jnp.where(causal_mask, jnp.float32(-jnp.inf), scores).astype(jnp.float32)
        attn = jax.nn.softmax(scores, axis=-1)
        out = jnp.einsum('bhts,bshd->bthd', attn, v).reshape(Bx, Tx, D)
        return out @ Wo.T

    def _L2_ffn_ref(x, Wr, W1, b1, W2, b2, fw1, fb1, fw2, fb2):
        import jax, jax.numpy as jnp
        import numpy as np
        E = 8
        TOP_K = 2
        CAP_FACTOR = 1.25
        MIN_CAP = 4
        SCORE_SCALE = 1.0

        def _ffn(x, w1, b1, w2, b2):
            return jax.nn.gelu(x @ w1 + b1, approximate=False) @ w2 + b2
        B, S, D = x.shape
        T = B * S
        x_flat = x.reshape(T, D)
        logits = x_flat @ Wr.T * SCORE_SCALE
        probs = jax.nn.softmax(logits, axis=-1)
        topk_scores, topk_experts = jax.lax.top_k(probs, TOP_K)
        topk_scores = topk_scores / jnp.clip(topk_scores.sum(-1, keepdims=True), 1e-09, None)
        cap = max(int(CAP_FACTOR * (T * TOP_K / E)), MIN_CAP)
        y_fb = _ffn(x_flat, fw1, fb1, fw2, fb2)
        y_flat = jnp.zeros_like(x_flat)
        fallback = jnp.zeros((T,), bool)
        tok_ids = jnp.arange(T, dtype=jnp.int32)
        for e in range(E):
            match = topk_experts == e
            elig = match.any(-1) & ~fallback
            pos = jnp.cumsum(elig) - 1
            kept = elig & (pos < cap)
            overflow = elig & (pos >= cap)
            slot = jnp.where(kept, pos, cap)
            buf = jnp.zeros((cap + 1,), jnp.int32).at[slot].set(tok_ids)
            vmask = jnp.zeros((cap + 1,), bool).at[slot].set(kept)
            idx = buf[:cap]
            valid = vmask[:cap]
            x_e = x_flat[idx]
            y_e = _ffn(x_e, W1[e], b1[e], W2[e], b2[e])
            w_tok = (topk_scores * match).sum(-1)
            w = jnp.where(valid, w_tok[idx], 0.0)
            y_flat = y_flat.at[idx].add(y_e * w[:, None])
            y_flat = jnp.where(overflow[:, None], y_fb, y_flat)
            fallback = fallback | overflow
        return y_flat.reshape(B, S, D)

    def _L3_attn_ref(x, W_qkv, b_qkv, W_proj, b_proj, proj_mat):
        import jax, jax.numpy as jnp
        import numpy as np
        EMBED_DIM = 256
        N_HEADS = 16
        HEAD_DIM = EMBED_DIM // N_HEADS
        N_FEATURES = 64
        EPS = 0.0001

        def softmax_kernel(data, projection_matrix, eps=EPS):
            data_normalizer = data.shape[-1] ** (-0.25)
            proj = jnp.einsum('bhnd,fd->bhnf', data, projection_matrix) * data_normalizer
            proj_max = jnp.max(proj, axis=-1, keepdims=True)
            return jnp.exp(proj - proj_max + eps)
        B, N, D = x.shape
        qkv = x @ W_qkv.T + b_qkv
        qkv = qkv.reshape(B, N, 3, N_HEADS, HEAD_DIM)
        qkv = jnp.transpose(qkv, (2, 0, 3, 1, 4))
        q, k, v = (qkv[0], qkv[1], qkv[2])
        q_prime = softmax_kernel(q, proj_mat)
        k_prime = softmax_kernel(k, proj_mat)
        kv = jnp.einsum('bhnf,bhnv->bhfv', k_prime, v)
        out = jnp.einsum('bhnf,bhfv->bhnv', q_prime, kv)
        k_sum = jnp.sum(k_prime, axis=2)
        normalizer = jnp.einsum('bhnf,bhf->bhn', q_prime, k_sum)[..., None]
        out = out / (normalizer + 1e-06)
        out = jnp.transpose(out, (0, 2, 1, 3)).reshape(B, N, D)
        return out @ W_proj.T + b_proj

    def _L3_ffn_ref(x, W_exp, b_exp, up_weights, up_bias, down_weights, W_con, b_con, down_bias):
        import jax, jax.numpy as jnp
        import numpy as np
        D_MODEL = 256
        EXPANSION = 4
        D_HIDDEN = D_MODEL * EXPANSION
        NUM_STAGES = int(np.log2(D_HIDDEN))

        def butterfly(y, weights, dim):
            lead = y.shape[:-1]
            for stage in range(weights.shape[0]):
                s = 2 ** stage
                nb = dim // (2 * s)
                yr = y.reshape(*lead, nb, 2, s)
                a = yr[..., 0, :]
                b = yr[..., 1, :]
                w = weights[stage].reshape(nb, s, 2, 2)
                na = w[..., 0, 0] * a + w[..., 0, 1] * b
                nb2 = w[..., 1, 0] * a + w[..., 1, 1] * b
                y = jnp.stack([na, nb2], axis=-2).reshape(*lead, dim)
            return y
        h = jnp.einsum('bsd,dh->bsh', x, W_exp) + b_exp
        h = butterfly(h, up_weights, D_HIDDEN)
        h = jax.nn.gelu(h + up_bias, approximate=False)
        h = butterfly(h, down_weights, D_HIDDEN)
        y = jnp.einsum('bsh,hd->bsd', h, W_con) + b_con
        return y + down_bias
    h = _L0_tok_ref(x, itok_BS_1_7, itok_BS_0_1439, L0_tok_hour_tab, L0_tok_wd_tab, L0_tok_t_w1, L0_tok_t_b1, L0_tok_t_gamma, L0_tok_t_beta, L0_tok_t_w2, L0_tok_t_b2, L0_tok_d_w1, L0_tok_d_b1, L0_tok_d_gamma, L0_tok_d_beta, L0_tok_d_w2, L0_tok_d_b2, L0_tok_proj_w, L0_tok_proj_b)
    h = h + _L0_attn_ref(_layernorm(h, axis=-1), L0_attn_wq, L0_attn_wk, L0_attn_wv, L0_attn_wo)
    h = h + _L0_ffn_ref(_layernorm(h, axis=-1), L0_ffn_m1, L0_ffn_m2, L0_ffn_mb, L0_ffn_w1, L0_ffn_w2, L0_ffn_b2)
    h = h + _L1_attn_ref(_layernorm(h, axis=-1), L1_attn_Wq, L1_attn_Wk, L1_attn_Wv, L1_attn_Wg, L1_attn_Wo)
    h = h + _L1_ffn_ref(_layernorm(h, axis=-1), L1_ffn_Win, L1_ffn_bin_, L1_ffn_W1, L1_ffn_b1, L1_ffn_W2, L1_ffn_b2, L1_ffn_Wout, L1_ffn_bout)
    h = h + _L2_attn_ref(_layernorm(h, axis=-1), L2_attn_Wq, L2_attn_Wk, L2_attn_Wv, L2_attn_Wo)
    h = h + _L2_ffn_ref(_layernorm(h, axis=-1), L2_ffn_Wr, L2_ffn_W1, L2_ffn_b1, L2_ffn_W2, L2_ffn_b2, L2_ffn_fw1, L2_ffn_fb1, L2_ffn_fw2, L2_ffn_fb2)
    h = h + _L3_attn_ref(_layernorm(h, axis=-1), L3_attn_W_qkv, L3_attn_b_qkv, L3_attn_W_proj, L3_attn_b_proj, L3_attn_proj_mat)
    h = h + _L3_ffn_ref(_layernorm(h, axis=-1), L3_ffn_W_exp, L3_ffn_b_exp, L3_ffn_up_weights, L3_ffn_up_bias, L3_ffn_down_weights, L3_ffn_W_con, L3_ffn_b_con, L3_ffn_down_bias)
    return h

_drawn_inputs = setup_inputs


def setup_inputs(seed=0):
    import zlib

    import numpy as np

    out = dict(_drawn_inputs(seed))
    spreads = {'L0_tok_t_b1': (0.0, 0.1),
     'L0_tok_t_gamma': (1.0, 0.2),
     'L0_tok_t_beta': (0.0, 0.582),
     'L0_tok_t_b2': (0.0, 0.1),
     'L0_tok_d_b1': (0.0, 0.1),
     'L0_tok_d_gamma': (1.0, 0.2),
     'L0_tok_d_beta': (0.0, 0.618),
     'L0_tok_d_b2': (0.0, 0.1),
     'L0_tok_proj_b': (0.0, 0.1),
     'L2_ffn_b1': (0.0, 0.8),
     'L2_ffn_b2': (0.0, 0.353),
     'L2_ffn_fb1': (0.0, 0.465),
     'L2_ffn_fb2': (0.0, 0.1),
     'L3_ffn_b_exp': (0.0, 0.1),
     'L3_ffn_up_bias': (0.0, 0.1),
     'L3_ffn_b_con': (0.0, 0.1),
     'L3_ffn_down_bias': (0.0, 0.1)}
    factors = {'L0_tok_hour_tab': 3.975,
     'L0_tok_wd_tab': 3.452,
     'L0_tok_d_w1': 3.643,
     'L1_attn_Wk': 3.224,
     'L1_attn_Wg': 8.0,
     'L1_ffn_bin_': 8.0,
     'L2_attn_Wq': 8.0,
     'L2_attn_Wk': 8.0,
     'L3_attn_b_qkv': 4.043,
     'L3_attn_b_proj': 2.752,
     'L3_attn_proj_mat': 64.0}
    for name, (base, spread) in spreads.items():
        noise = np.random.default_rng([zlib.crc32(name.encode()), seed]).standard_normal(out[name].shape)
        drawn = base * np.exp(spread * noise) if base else spread * noise
        out[name] = jnp.asarray(drawn.astype(out[name].dtype))
    for name, factor in factors.items():
        out[name] = (out[name] * factor).astype(out[name].dtype)
    return out
```

```python
from contextlib import ExitStack

import concourse.bass as bass
import numpy as np
from concourse import mybir
from concourse.alu_op_type import AluOpType as ALU

F32 = mybir.dt.float32
I32 = mybir.dt.int32
U8 = mybir.dt.uint8
BF16 = mybir.dt.bfloat16
ACT = mybir.ActivationFunctionType
X = mybir.AxisListType.X

P = 128
D = 256
KD = D // P
B, S = 8, 512
TILES = B * S // P
TPB = S // P
LN_EPS = 1e-5
CREDIT = 64


class Chain:

    def __init__(self, eng, sem):
        self.eng, self.sem, self.n = eng, sem, 0

    def restart(self):
        self.eng.sem_clear(self.sem)
        self.n = 0

    def link(self, ins):
        self.n += 1
        ins.then_inc(self.sem, 1)
        self.eng.wait_ge(self.sem, self.n)


class Stage:

    banks = []

    def __init__(self, nc, name):
        self.nc, self.name, self.ctx, self.taken = nc, name, ExitStack(), 0
        self.sem_ctx, self.sems = ExitStack(), []

    def __enter__(self):
        self.ctx.__enter__()
        return self

    def __exit__(self, *e):
        self.ctx.close()
        if self.sems:
            with self.nc.Block() as block:
                @block.sync
                def _(sp):
                    for sem in self.sems:
                        sp.sem_clear(sem)
        self.sem_ctx.close()

    def sb(self, name, shape, dt=F32):
        return self.ctx.enter_context(self.nc.sbuf_tensor(f"{self.name}_sb_{name}", shape, dt))

    def ps(self, shape):
        bank = Stage.banks[self.taken]
        self.taken += 1
        view = bank[0:shape[0], 0:int(np.prod(shape[1:]))]
        return view.rearrange("p (b n) -> p b n", b=shape[1]) if len(shape) == 3 else view

    def sem(self, name):
        self.sems.append(self.sem_ctx.enter_context(self.nc.semaphore(f"{self.name}_sem_{name}")))
        return self.sems[-1]


def pairs(eng, body):
    body(0, True, False)
    with eng.Fori(1, TILES // 2 - 1) as i:
        body(i, False, False)
    body(TILES // 2 - 1, False, True)


def norm_stage(nc, name, h, xnT, ident):
    with Stage(nc, name) as st:
        stats = st.sb("stats", [P, TILES, 6])
        mv = st.sb("mv", [P, TILES, 2])
        std = st.sb("std", [P, TILES])
        rstd = st.sb("rstd", [P, TILES])
        eps = st.sb("eps", [P, 1])
        xn = st.sb("xn", [P, 2, TPB, D])
        ps = [st.ps([P, S]) for k in range(2 * KD)]
        eps_set, s_dve = st.sem("eps_set"), st.sem("dve")
        mv_ready, std_ready, xn_ready = st.sem("mv_ready"), st.sem("std_ready"), st.sem("xn_ready")
        xnT_full, xnT_read = st.sem("xnT_full"), st.sem("xnT_read")
        block = st.ctx.enter_context(nc.Block())

        @block.vector
        def _(dve):
            ch = Chain(dve, s_dve)
            dve.memset(eps[:, :], LN_EPS).then_inc(eps_set, 1)
            for t in range(TILES):
                ins = dve.bn_stats(stats[:, t, :], h[:, t, :])
            ch.link(ins)
            for t in range(TILES):
                ins = dve.bn_aggr(mv[:, t, :], stats[:, t, :])
            ch.link(ins)
            dve.sem_inc(mv_ready, 1)
            dve.wait_ge(std_ready, 1)
            ch.link(dve.reciprocal(rstd[:, :], std[:, :]))
            flat = mv[:, :, :].rearrange("p t c -> p (t c)")
            with dve.Fori(0, B // 2) as i:
                for u in range(2):
                    b = i * 2 + u
                    dve.wait_ge(xnT_full, CREDIT + b - 1)
                    for t in range(TPB):
                        n = b * TPB + t
                        ins = dve.tensor_scalar(xn[:, u, t, :], h[:, n, :], flat[:, bass.ds(n * 2, 1)],
                                                rstd[:, bass.ds(n, 1)], ALU.subtract, ALU.mult)
                    ins.then_inc(xn_ready, 1)

        @block.tensor
        def _(pe):
            pe.sem_inc(xnT_full, CREDIT)
            with pe.Fori(0, B // 2) as i:
                for u in range(2):
                    b = i * 2 + u
                    pe.wait_ge(xn_ready, b + 1)
                    pe.wait_ge(xnT_read, CREDIT + b - 1)
                    for k in range(KD):
                        for t in range(TPB):
                            ins = pe.transpose(ps[2 * u + k][:, t * P:(t + 1) * P],
                                               xn[:, u, t, k * P:(k + 1) * P], ident[:, :])
                    ins.then_inc(xnT_full, 1)

        @block.scalar
        def _(act):
            act.sem_inc(xnT_read, CREDIT)
            act.wait_ge(eps_set, 1)
            act.wait_ge(mv_ready, 1)
            act.activation(std[:, :], mv[:, :, 1], ACT.Sqrt, bias=eps[:, 0:1]).then_inc(std_ready, 1)
            with act.Fori(0, B // 2) as i:
                for u in range(2):
                    b = i * 2 + u
                    act.wait_ge(xnT_full, CREDIT + b + 1)
                    for k in range(KD):
                        ins = act.activation(xnT[:, k, bass.ds(b * S, S)], ps[2 * u + k][:, :], ACT.Copy)
                    ins.then_inc(xnT_read, 1)


def l0_attn_stage(nc, h, xnT, ident, wq, wk, wv, wo):
    C, HD, G, GT = 16, 64, 4, 32
    GS = C * GT
    R = GS // P
    NP = C // 2
    SCALE = HD ** -0.5
    JOBS = 6
    with Stage(nc, "l0a") as st:
        wq_sb, wk_sb, wv_sb = (st.sb(n, [P, KD, C * HD]) for n in ("wq", "wk", "wv"))
        wo_sb = st.sb("wo", [P, NP, D])
        xs = st.sb("xs", [P, 2, KD, P])
        qT = st.sb("qT", [HD, 2, G, GS])
        kT = st.sb("kT", [HD, 2, G, GS])
        v = st.sb("v", [P, 2, G, R, HD])
        p = st.sb("p", [P, 2, R, GS])
        pT = st.sb("pT", [P, 2, R, GS])
        oT = st.sb("oT", [P, 2, NP, P])
        nmx = st.sb("nmx", [P, 2, R])
        sums = st.sb("sums", [P, 2, R])
        rsum = st.sb("rsum", [P, 2, R])
        ps_proj = [st.ps([P, 512]) for k in range(2)]
        ps_s = [st.ps([P, GS]) for k in range(2)]
        ps_t = [st.ps([P, GS]) for k in range(2)]
        ps_o = st.ps([HD, GS])
        ps_y = st.ps([P, D])
        w_in, s_dve = st.sem("w_in"), st.sem("dve")
        xs_ready, proj_full = st.sem("xs_ready"), st.sem("proj_full")
        proj_read = [st.sem(f"proj_read{k}") for k in range(2)]
        s_full, nmx_ready, exp_done = st.sem("s_full"), st.sem("nmx_ready"), st.sem("exp_done")
        p_ready, t_full = st.sem("p_ready"), st.sem("t_full")
        pT_ready = [st.sem(f"pT_ready{k}") for k in range(2)]
        o_full, oT_ready, y_full, y_added = (st.sem(n) for n in ("o_full", "oT_ready", "y_full", "y_added"))
        block = st.ctx.enter_context(nc.Block())

        @block.sync
        def _(sp):
            for dst, src in ((wq_sb, wq), (wk_sb, wk), (wv_sb, wv), (wo_sb, wo)):
                sp.dma_start(dst[:, :, :], src).then_inc(w_in, 16)

        @block.gpsimd
        def _(pool):
            with pool.Fori(0, TILES // 2) as i:
                for u in range(2):
                    n = i * 2 + u
                    pool.wait_ge(proj_full, CREDIT + (n - 1) * JOBS)
                    pool.tensor_copy(xs[:, u, :, :], xnT[:, :, bass.ds(n * P, P)]).then_inc(xs_ready, 1)

        @block.tensor
        def _(pe):
            for s in (proj_full, s_full, t_full, o_full, y_full):
                pe.sem_inc(s, CREDIT)
            pe.wait_ge(w_in, 4 * 16)

            def project(n, u, jobs):
                pe.wait_ge(xs_ready, n + 1)
                for j in jobs:
                    pe.wait_ge(proj_read[j % 2], CREDIT + n * (JOBS // 2) + j // 2)
                    for m in range(4 if j < 4 else 1):
                        for k in range(KD):
                            if j < 4:
                                w = (wq_sb, wk_sb)[j // 2]
                                c = (4 * (j % 2) + m) * P
                                ins = pe.matmul(ps_proj[j % 2][:, m * P:(m + 1) * P],
                                                w[:, k, c:c + P], xs[:, u, k, :],
                                                start=k == 0, stop=k == KD - 1)
                            else:
                                ins = pe.matmul(ps_proj[j % 2][:, :], xs[:, u, k, :],
                                                wv_sb[:, k, (j - 4) * 512:(j - 3) * 512],
                                                start=k == 0, stop=k == KD - 1)
                    ins.then_inc(proj_full, 1)

            def scores(n, u, g):
                if g == 0:
                    for k in range(2):
                        pe.wait_ge(proj_read[k], CREDIT + n * (JOBS // 2) + 2)
                for r in range(R):
                    pe.wait_ge(exp_done, CREDIT + (n * G + g) * R + r - 1)
                    pe.matmul(ps_s[r % 2][:, :], qT[:, u, g, r * P:(r + 1) * P], kT[:, u, g, :],
                              start=True, stop=True).then_inc(s_full, 1)

            def result(n, u):
                pe.wait_ge(oT_ready, CREDIT + (n + 1) * G)
                pe.wait_ge(y_added, CREDIT + n)
                for k in range(NP):
                    ins = pe.matmul(ps_y[:, :], oT[:, u, k, :], wo_sb[:, k, :],
                                    start=k == 0, stop=k == NP - 1)
                ins.then_inc(y_full, 1)

            def body(i, first, last):
                for u in range(2):
                    n = i * 2 + u
                    behind = not (last and u == 1)
                    for g in range(G):
                        if g + 1 < G:
                            scores(n, u, g + 1)
                        elif behind:
                            scores(n + 1, 1 - u, 0)
                        pe.wait_ge(p_ready, n * G + g + 1)
                        for kt in range(R):
                            pe.wait_ge(pT_ready[kt % 2], CREDIT + (n * G + g) * 2 + kt // 2)
                            for r in range(R):
                                ins = pe.transpose(ps_t[kt % 2][:, r * P:(r + 1) * P],
                                                   p[:, g % 2, r, kt * P:(kt + 1) * P], ident[:, :])
                            ins.then_inc(t_full, 1)
                        if g == 0:
                            if not (first and u == 0):
                                result(n - 1, 1 - u)
                            for k in range(2):
                                pe.wait_ge(proj_read[k], CREDIT + (n + 1) * (JOBS // 2))
                        elif behind:
                            project(n + 1, 1 - u, (2 * g - 2, 2 * g - 1))
                        pe.wait_ge(oT_ready, CREDIT + n * G + g)
                        for kt in range(R):
                            pe.wait_ge(pT_ready[kt % 2], CREDIT + (n * G + g) * 2 + kt // 2 + 1)
                            ins = pe.matmul(ps_o[:, :], v[:, u, g, kt, :], pT[:, g % 2, kt, :],
                                            start=kt == 0, stop=kt == R - 1)
                        ins.then_inc(o_full, 1)

            project(0, 0, range(JOBS))
            scores(0, 0, 0)
            pairs(pe, body)
            result(TILES - 1, 1)

        @block.scalar
        def _(act):
            act.sem_inc(exp_done, CREDIT)
            act.sem_inc(pT_ready[1], CREDIT)

            def take_qk(n, u, jobs):
                act.wait_ge(s_full, CREDIT + (n - 1) * G * R)
                for j in jobs:
                    act.wait_ge(proj_full, CREDIT + n * JOBS + j + 1)
                    dst = (qT, kT)[j // 2][:, u, :, :].rearrange("p g (c t) -> p g c t", t=GT)
                    for odd in range(2):
                        src = ps_proj[j % 2][odd * HD:(odd + 1) * HD, :].rearrange(
                            "p (m g t) -> p g m t", m=4, t=GT)
                        c = 8 * (j % 2) + odd
                        ins = act.activation(dst[:, :, c:c + 7:2, :], src, ACT.Copy,
                                             scale=SCALE if j < 2 else 1.0)
                    ins.then_inc(proj_read[j % 2], 1)

            def exps(n, g, rows):
                act.wait_ge(t_full, CREDIT + (n * G + g - 1) * R)
                for r in rows:
                    act.wait_ge(nmx_ready, (n * G + g) * R + r + 1)
                    act.activation(p[:, g % 2, r, :], ps_s[r % 2][:, :], ACT.Exp,
                                   bias=nmx[:, g % 2, r:r + 1],
                                   accum_out=sums[:, g % 2, r:r + 1]).then_inc(exp_done, 1)

            def body(i, first, last):
                for u in range(2):
                    n = i * 2 + u
                    behind = not (last and u == 1)
                    for g in range(G):
                        for kt in (1, 3):
                            rows = (0, 1, 2) if kt == 1 else (3,)
                            if g + 1 < G:
                                exps(n, g + 1, rows)
                            elif behind:
                                exps(n + 1, 0, rows)
                            act.wait_ge(t_full, CREDIT + (n * G + g) * R + kt + 1)
                            act.wait_ge(o_full, CREDIT + n * G + g - 1)
                            act.activation(pT[:, g % 2, kt, :], ps_t[1][:, :], ACT.Copy)\
                                .then_inc(pT_ready[1], 1)
                        if g in (1, 2) and behind:
                            take_qk(n + 1, 1 - u, (2 * g - 2, 2 * g - 1))

            take_qk(0, 0, range(4))
            exps(0, 0, range(R))
            pairs(act, body)

        @block.vector
        def _(dve):
            ch = Chain(dve, s_dve)
            for s in (*proj_read, pT_ready[0], oT_ready, y_added):
                dve.sem_inc(s, CREDIT)

            def take_v(n, u):
                dve.wait_ge(o_full, CREDIT + (n - 1) * G)
                for j in (4, 5):
                    dve.wait_ge(proj_full, CREDIT + n * JOBS + j + 1)
                    src = ps_proj[j % 2][:, :].rearrange("p (k c d) -> p k c d", k=2, d=HD)
                    for g in range(G):
                        for c4 in range(4):
                            ins = dve.tensor_copy(
                                v[c4 * GT:(c4 + 1) * GT, u, g, 2 * (j - 4):2 * (j - 4) + 2, :],
                                src[g * GT:(g + 1) * GT, :, c4, :])
                    ins.then_inc(proj_read[j % 2], 1)

            def maxima(n, g, rows):
                dve.wait_ge(exp_done, CREDIT + (n * G + g - 1) * R)
                for r in rows:
                    dve.wait_ge(s_full, CREDIT + (n * G + g) * R + r + 1)
                    dve.tensor_reduce(nmx[:, g % 2, r:r + 1], ps_s[r % 2][:, :], X, ALU.max,
                                      negate=True).then_inc(nmx_ready, 1)

            def add(n):
                dve.wait_ge(y_full, CREDIT + n + 1)
                dve.tensor_tensor(h[:, n, :], h[:, n, :], ps_y[:, :], ALU.add).then_inc(y_added, 1)

            def body(i, first, last):
                ch.restart()
                for u in range(2):
                    n = i * 2 + u
                    behind = not (last and u == 1)
                    for g in range(G):
                        if g + 1 < G:
                            maxima(n, g + 1, (0, 1))
                        elif behind:
                            maxima(n + 1, 0, (0, 1))
                        dve.wait_ge(exp_done, CREDIT + (n * G + g + 1) * R)
                        ch.link(dve.reciprocal(rsum[:, g % 2, :], sums[:, g % 2, :]))
                        for r in range(R):
                            ins = dve.tensor_scalar(p[:, g % 2, r, :], p[:, g % 2, r, :],
                                                    rsum[:, g % 2, r:r + 1], None, ALU.mult)
                        ins.then_inc(p_ready, 1)
                        for kt in (0, 2):
                            if g + 1 < G:
                                maxima(n, g + 1, (2 + kt // 2,))
                            elif behind:
                                maxima(n + 1, 0, (2 + kt // 2,))
                            dve.wait_ge(t_full, CREDIT + (n * G + g) * R + kt + 1)
                            dve.wait_ge(o_full, CREDIT + n * G + g - 1)
                            dve.tensor_copy(pT[:, g % 2, kt, :], ps_t[0][:, :]).then_inc(pT_ready[0], 1)
                        if g == 0 and not (first and u == 0):
                            add(n - 1)
                        if g + 1 == G and behind:
                            take_v(n + 1, 1 - u)
                        if g == 0:
                            dve.wait_ge(y_full, CREDIT + n - 1)
                        dve.wait_ge(o_full, CREDIT + n * G + g + 1)
                        src = ps_o[:, :].rearrange("p (c o t) -> p c o t", o=2, t=GT)
                        for odd in range(2):
                            ins = dve.tensor_copy(oT[odd * HD:(odd + 1) * HD, u, :, g * GT:(g + 1) * GT],
                                                  src[:, :, odd, :])
                        ins.then_inc(oT_ready, 1)

            take_v(0, 0)
            maxima(0, 0, range(R))
            pairs(dve, body)
            add(TILES - 1)


def token_stage(nc, h, ident, a):
    E = 64
    NI, NF = 64, 4
    ENC = 2 * TPB
    MAGIC = 1.5 * 2 ** 23
    with Stage(nc, "tok") as st:
        tab = st.sb("tab", [NI, P])
        w1 = st.sb("w1", [NF + 1, P])
        w2 = st.sb("w2", [P, P])
        proj = st.sb("proj", [P, KD, D])
        projb = st.sb("projb", [P, D])
        cols = st.sb("cols", [P, 8])
        gamma, beta, b2, index, last, turn, minus_turn = (cols[:, k:k + 1] for k in range(7))
        fcols = st.sb("fcols", [NF, 3])
        idx = st.sb("idx", [NI + NF, 2, S], I32)
        hot = st.sb("hot", [NI, 2, S])
        ang = st.sb("ang", [NF, 2, S])
        whole = st.sb("whole", [NF, 2, S])
        feat = st.sb("feat", [NF + 1, 2, S])
        stats = st.sb("stats", [P, 2, ENC, 6])
        mv = st.sb("mv", [P, 2, ENC, 2])
        std = st.sb("std", [P, 2, ENC])
        rstd = st.sb("rstd", [P, 2, ENC])
        xh = st.sb("xh", [P, 2, TPB, P])
        enc = st.sb("enc", [P, 2, S])
        comb = st.sb("comb", [P, 2, KD, S])
        ps_e, ps_t, ps_w, ps_m = (st.ps([P, S]) for k in range(4))
        ps_y = [st.ps([P, 2, D]) for k in range(2)]
        w_in, s_dve = st.sem("w_in"), st.sem("dve")
        idx_in = [st.sem(f"idx_in{u}") for u in range(2)]
        hot_ready, ang_ready, feat_ready = st.sem("hot_ready"), st.sem("ang_ready"), st.sem("feat_ready")
        e_full, mv_ready, std_ready, xh_ready = (st.sem(n) for n in ("e_full", "mv_ready", "std_ready", "xh_ready"))
        t_full, enc_ready, w_full, m_full = (st.sem(n) for n in ("t_full", "enc_ready", "w_full", "m_full"))
        comb_ready, y_full, y_read, ones_set = (st.sem(n) for n in ("comb_ready", "y_full", "y_read", "ones_set"))
        block = st.ctx.enter_context(nc.Block())

        @block.sync
        def _(sp):
            loads = ((tab[:, :], a["tab"]), (w1[:, :], a["tok_w1"]), (w2[:, :], a["tok_w2"]),
                     (proj[:, :, :], a["proj_w"]), (projb[:, :], a["proj_b"]),
                     (cols[:, :], a["tok_cols"]), (fcols[:, :], a["c_fcols"]))
            for dst, src in loads:
                sp.dma_start(dst, src).then_inc(w_in, 16)
            with sp.Fori(0, B // 2) as i:
                for u in range(2):
                    b = i * 2 + u
                    sp.wait_ge(ang_ready, CREDIT + b - 1)
                    sp.dma_start(idx[:, u, :], a["idx"][:, bass.ds(b * S, S)]).then_inc(idx_in[u], 16)

        @block.vector
        def _(dve):
            ch = Chain(dve, s_dve)
            dve.memset(feat[:, :, :], 1.0).then_inc(ones_set, 1)
            for s in (ang_ready, y_read):
                dve.sem_inc(s, CREDIT)
            dve.wait_ge(w_in, 7 * 16)
            with dve.Fori(0, B // 2) as i:
                ch.restart()
                for u in range(2):
                    b = i * 2 + u
                    dve.wait_ge(idx_in[u], 16 * (i + 1))
                    dve.wait_ge(m_full, CREDIT + b - 1)
                    dve.tensor_scalar(hot[:, u, :], idx[0:NI, u, :], last[0:NI, :], index[0:NI, :],
                                      ALU.min, ALU.is_equal).then_inc(hot_ready, 1)
                    ch.link(dve.tensor_scalar(ang[:, u, :], idx[NI:NI + NF, u, :], fcols[:, 0:1],
                                              fcols[:, 1:2], ALU.mult, ALU.add))
                    ch.link(dve.tensor_scalar(whole[:, u, :], ang[:, u, :], turn[0:NF, :], MAGIC,
                                              ALU.mult, ALU.add))
                    ch.link(dve.tensor_scalar(whole[:, u, :], whole[:, u, :], MAGIC, None, ALU.subtract))
                    ch.link(dve.scalar_tensor_tensor(out=ang[:, u, :], in0=whole[:, u, :],
                                                     scalar=minus_turn[0:NF, :], in1=ang[:, u, :],
                                                     op0=ALU.mult, op1=ALU.add))
                    dve.sem_inc(ang_ready, 1)
                for u in range(2):
                    b = i * 2 + u
                    dve.wait_ge(e_full, CREDIT + b + 1)
                    for t in range(ENC):
                        ins = dve.bn_stats(stats[:, u, t, :], ps_e[:, t * E:(t + 1) * E])
                    ch.link(ins)
                    for t in range(ENC):
                        ins = dve.bn_aggr(mv[:, u, t, :], stats[:, u, t, :])
                    ch.link(ins)
                    dve.sem_inc(mv_ready, 1)
                    dve.wait_ge(std_ready, b + 1)
                    ch.link(dve.reciprocal(rstd[:, u, :], std[:, u, :]))
                    dve.wait_ge(t_full, CREDIT + b - 1)
                    for t in range(ENC):
                        ins = dve.tensor_scalar(xh[:, u, t // 2, (t % 2) * E:(t % 2 + 1) * E],
                                                ps_e[:, t * E:(t + 1) * E], mv[:, u, t, 0:1],
                                                rstd[:, u, t:t + 1], ALU.subtract, ALU.mult)
                    ins.then_inc(xh_ready, 1)
                for u in range(2):
                    b = i * 2 + u
                    for y in range(2):
                        dve.wait_ge(y_full, CREDIT + b * 2 + y + 1)
                        dve.tensor_tensor(h[:, bass.ds(b * TPB + 2 * y, 2), :], ps_y[y][:, :, :],
                                          projb[:, :].unsqueeze(1).to_broadcast([P, 2, D]),
                                          ALU.add).then_inc(y_read, 1)

        @block.scalar
        def _(act):
            act.sem_inc(enc_ready, CREDIT)
            act.wait_ge(w_in, 7 * 16)
            act.wait_ge(ones_set, 1)
            with act.Fori(0, B // 2) as i:
                for u in range(2):
                    b = i * 2 + u
                    act.wait_ge(ang_ready, CREDIT + b + 1)
                    act.wait_ge(e_full, CREDIT + b - 1)
                    act.activation(feat[0:NF, u, :], ang[:, u, :], ACT.Sin,
                                   scale=fcols[:, 2:3]).then_inc(feat_ready, 1)
                for u in range(2):
                    act.wait_ge(mv_ready, i * 2 + u + 1)
                    act.activation(std[:, u, :], mv[:, u, :, 1], ACT.Sqrt,
                                   bias=cols[:, 7:8]).then_inc(std_ready, 1)
                for u in range(2):
                    b = i * 2 + u
                    act.wait_ge(t_full, CREDIT + b + 1)
                    act.wait_ge(w_full, CREDIT + b - 1)
                    act.activation(enc[:, u, :], ps_t[:, :], ACT.Gelu, scale=gamma,
                                   bias=beta).then_inc(enc_ready, 1)
                    act.wait_ge(y_full, CREDIT + (b - 1) * 2)
                    act.wait_ge(m_full, CREDIT + b + 1)
                    act.activation(comb[:, u, 0, :], ps_m[:, :], ACT.Copy)
                    act.wait_ge(w_full, CREDIT + b + 1)
                    act.activation(comb[:, u, 1, :], ps_w[:, :], ACT.Identity,
                                   bias=b2).then_inc(comb_ready, 1)

        @block.tensor
        def _(pe):
            for s in (e_full, t_full, w_full, m_full, y_full):
                pe.sem_inc(s, CREDIT)
            pe.sem_inc(comb_ready, CREDIT)
            pe.sem_inc(xh_ready, CREDIT)
            pe.wait_ge(w_in, 7 * 16)
            with pe.Fori(0, B // 2) as i:
                for u in range(2):
                    b = i * 2 + u
                    pe.wait_ge(feat_ready, b + 1)
                    pe.wait_ge(xh_ready, CREDIT + b)
                    for t in range(TPB):
                        ins = pe.matmul(ps_e[:, t * P:(t + 1) * P], feat[:, u, t * P:(t + 1) * P],
                                        w1[:, :], start=True, stop=True)
                    ins.then_inc(e_full, 1)
                for u in range(2):
                    b = i * 2 + u
                    pe.wait_ge(hot_ready, b + 1)
                    pe.wait_ge(comb_ready, CREDIT + b)
                    pe.matmul(ps_m[:, :], tab[:, :], hot[:, u, :], start=True, stop=True).then_inc(m_full, 1)
                    pe.wait_ge(xh_ready, CREDIT + b + 1)
                    pe.wait_ge(enc_ready, CREDIT + b)
                    for t in range(TPB):
                        ins = pe.transpose(ps_t[:, t * P:(t + 1) * P], xh[:, u, t, :], ident[:, :])
                    ins.then_inc(t_full, 1)
                    pe.wait_ge(enc_ready, CREDIT + b + 1)
                    pe.matmul(ps_w[:, :], w2[:, :], enc[:, u, :], start=True, stop=True).then_inc(w_full, 1)
                    pe.wait_ge(comb_ready, CREDIT + b + 1)
                    for y in range(2):
                        pe.wait_ge(y_read, CREDIT + b * 2 + y - 1)
                        for t in (2 * y, 2 * y + 1):
                            for k in range(KD):
                                ins = pe.matmul(ps_y[y][:, t % 2, :], comb[:, u, k, t * P:(t + 1) * P],
                                                proj[:, k, :], start=k == 0, stop=k == KD - 1)
                        ins.then_inc(y_full, 1)


def l0_ffn_stage(nc, h, xnT, ident, a):
    G, U, DL = 16, 64, 64
    HF = G * U // 2
    KH = G * U // P
    with Stage(nc, "l0f") as st:
        m1 = st.sb("m1", [P, KD, DL])
        m2 = st.sb("m2", [DL + 1, 2 * HF])
        w1 = st.sb("w1", [P, KD, 2 * HF])
        w2 = st.sb("w2", [P, KH, D])
        b2 = st.sb("b2", [P, D])
        rank_in = st.sb("rank_in", [P, U])
        rank = st.sb("rank", [P, U], BF16)
        xs = st.sb("xs", [P, 2, KD, P])
        lrT = st.sb("lrT", [DL + 1, 2, P])
        top = st.sb("top", [P, 2, G // 2])
        ranked = st.sb("ranked", [P, 2, HF], BF16)
        best = st.sb("best", [P, 2, G // 2], BF16)
        hot = st.sb("hot", [P, 2, HF], BF16)
        hid = st.sb("hid", [P, 2, 2 * HF])
        hidT = st.sb("hidT", [P, 2, KH, P])
        ps_r = st.ps([DL, P])
        ps_l = [st.ps([P, HF]) for k in range(2)]
        ps_m = [st.ps([P, HF]) for k in range(2)]
        ps_t = [st.ps([P, 4 * P]) for k in range(2)]
        ps_y = st.ps([P, D])
        w_in, s_dve, ones_set = st.sem("w_in"), st.sem("dve"), st.sem("ones_set")
        xs_ready, r_full, lrT_ready = st.sem("xs_ready"), st.sem("r_full"), st.sem("lrT_ready")
        l_full, m_full, hid_ready = st.sem("l_full"), st.sem("m_full"), st.sem("hid_ready")
        t_full, hidT_ready, y_full, y_added = (st.sem(n) for n in ("t_full", "hidT_ready", "y_full", "y_added"))
        l_read = st.sem("l_read")
        block = st.ctx.enter_context(nc.Block())

        @block.sync
        def _(sp):
            for dst, src in ((m1[:, :, :], a["m1"]), (m2[:, :], a["m2"]), (w1[:, :, :], a["w1_0"]),
                             (w2[:, :, :], a["w2_0"]), (b2[:, :], a["b2_0"]), (rank_in[:, :], a["c_rank"])):
                sp.dma_start(dst, src).then_inc(w_in, 16)

        @block.gpsimd
        def _(pool):
            pool.memset(lrT[DL:DL + 1, :, :], 1.0).then_inc(ones_set, 1)
            pool.wait_ge(ones_set, 1)
            pool.wait_ge(w_in, 6 * 16)
            with pool.Fori(0, TILES // 2) as i:
                for u in range(2):
                    n = i * 2 + u
                    pool.tensor_tensor(h[:, n, :], h[:, n, :], b2[:, :], ALU.add)
                    pool.wait_ge(m_full, CREDIT + (n - 1) * 2)
                    pool.tensor_copy(xs[:, u, :, :], xnT[:, :, bass.ds(n * P, P)]).then_inc(xs_ready, 1)

        @block.tensor
        def _(pe):
            for s in (r_full, l_full, m_full, t_full, y_full):
                pe.sem_inc(s, CREDIT)
            pe.wait_ge(w_in, 6 * 16)
            pe.wait_ge(ones_set, 1)
            def low_rank(n, u):
                pe.wait_ge(xs_ready, n + 1)
                pe.wait_ge(lrT_ready, CREDIT + n)
                for k in range(KD):
                    ins = pe.matmul(ps_r[:, :], m1[:, k, :], xs[:, u, k, :], start=k == 0, stop=k == KD - 1)
                ins.then_inc(r_full, 1)

            def first_layer(n, u, f):
                pe.wait_ge(hid_ready, CREDIT + (n - 1) * 2 + f + 1)
                for k in range(KD):
                    ins = pe.matmul(ps_m[f][:, :], xs[:, u, k, :], w1[:, k, f * HF:(f + 1) * HF],
                                    start=k == 0, stop=k == KD - 1)
                ins.then_inc(m_full, 1)
                if f == 0:
                    pe.wait_ge(lrT_ready, CREDIT + n + 1)
                pe.wait_ge(l_read, CREDIT + (n - 1) * 2 + f + 1)
                pe.matmul(ps_l[f][:, :], lrT[:, u, :], m2[:, f * HF:(f + 1) * HF],
                          start=True, stop=True).then_inc(l_full, 1)

            def body(i, first, last):
                for u in range(2):
                    n = i * 2 + u
                    behind = not (last and u == 1)
                    if behind:
                        low_rank(n + 1, 1 - u)
                    for f in range(2):
                        pe.wait_ge(hid_ready, CREDIT + n * 2 + f + 1)
                        pe.wait_ge(hidT_ready, CREDIT + (n - 1) * 2 + f + 1)
                        for k in range(4):
                            ins = pe.transpose(ps_t[f][:, k * P:(k + 1) * P],
                                               hid[:, u, f * HF + k * P:f * HF + (k + 1) * P], ident[:, :])
                        ins.then_inc(t_full, 1)
                        if behind:
                            first_layer(n + 1, 1 - u, f)
                    pe.wait_ge(y_added, CREDIT + n)
                    for k in range(KH):
                        if k % 4 == 0:
                            pe.wait_ge(hidT_ready, CREDIT + n * 2 + k // 4 + 1)
                        ins = pe.matmul(ps_y[:, :], hidT[:, u, k, :], w2[:, k, :],
                                        start=k == 0, stop=k == KH - 1)
                    ins.then_inc(y_full, 1)

            low_rank(0, 0)
            for f in range(2):
                first_layer(0, 0, f)
            pairs(pe, body)

        @block.scalar
        def _(act):
            act.sem_inc(lrT_ready, CREDIT)
            act.sem_inc(hidT_ready, CREDIT)

            def take_low_rank(n, u):
                act.wait_ge(r_full, CREDIT + n + 1)
                act.wait_ge(l_full, CREDIT + (n - 1) * 2)
                act.activation(lrT[0:DL, u, :], ps_r[:, :], ACT.Copy).then_inc(lrT_ready, 1)

            def body(i, first, last):
                for u in range(2):
                    n = i * 2 + u
                    if not (last and u == 1):
                        take_low_rank(n + 1, 1 - u)
                    act.wait_ge(y_full, CREDIT + n - 1)
                    for f in range(2):
                        act.wait_ge(t_full, CREDIT + n * 2 + f + 1)
                        act.activation(hidT[:, u, 4 * f:4 * f + 4, :], ps_t[f][:, :].rearrange(
                            "p (k t) -> p k t", k=4), ACT.Copy).then_inc(hidT_ready, 1)

            take_low_rank(0, 0)
            pairs(act, body)

        @block.vector
        def _(dve):
            ch = Chain(dve, s_dve)
            for s in (hid_ready, l_read, y_added):
                dve.sem_inc(s, CREDIT)
            grouped = lambda x: x.rearrange("p (g u) -> p g u", u=U)
            dve.wait_ge(w_in, 6 * 16)
            ch.link(dve.tensor_copy(rank[:, :], rank_in[:, :]))

            def add(n):
                dve.wait_ge(y_full, CREDIT + n + 1)
                dve.tensor_tensor(h[:, n, :], h[:, n, :], ps_y[:, :], ALU.add).then_inc(y_added, 1)

            def body(i, first, last):
                ch.restart()
                for u in range(2):
                    n = i * 2 + u
                    for f in range(2):
                        over = lambda x: x[:, f, :].unsqueeze(2).to_broadcast([P, G // 2, U])
                        dve.wait_ge(l_full, CREDIT + n * 2 + f + 1)
                        ch.link(dve.tensor_reduce(top[:, f, :], grouped(ps_l[f][:, :]), X, ALU.max))
                        ch.link(dve.tensor_tensor(grouped(hot[:, f, :]), grouped(ps_l[f][:, :]),
                                                  over(top), ALU.is_ge))
                        dve.sem_inc(l_read, 1)
                        ch.link(dve.tensor_tensor(
                            grouped(ranked[:, f, :]), grouped(hot[:, f, :]),
                            rank[:, :].unsqueeze(1).to_broadcast([P, G // 2, U]), ALU.mult))
                        ch.link(dve.tensor_reduce(best[:, f, :], grouped(ranked[:, f, :]), X, ALU.max))
                        ch.link(dve.tensor_tensor(grouped(hot[:, f, :]), grouped(ranked[:, f, :]),
                                                  over(best), ALU.is_equal))
                        dve.wait_ge(m_full, CREDIT + n * 2 + f + 1)
                        dve.wait_ge(t_full, CREDIT + (n - 1) * 2)
                        dve.scalar_tensor_tensor(out=hid[:, u, f * HF:(f + 1) * HF], in0=ps_m[f][:, :],
                                                 scalar=0.0, in1=hot[:, f, :], op0=ALU.max,
                                                 op1=ALU.mult).then_inc(hid_ready, 1)
                        if f == 0 and not (first and u == 0):
                            add(n - 1)

            pairs(dve, body)
            add(TILES - 1)


def l1_attn_stage(nc, h, xnT, ident, a):
    H, C = 8, 4
    LEVELS = P.bit_length() - 1
    NB = B // 2
    JOBS = 9
    EPS2 = 1e-24
    UP, TINY, CLEAN = 2.0 ** 40, 2.0 ** -40, (5, 6, 7)
    with Stage(nc, "l1a") as st:
        w = st.sb("w", [P, 2, 4, KD, P])
        wo = st.sb("wo", [P, 2, D])
        ones = st.sb("ones", [P, P])
        diag = st.sb("diag", [P, P])
        masks = st.sb("masks", [P, LEVELS, P], U8)
        xs = st.sb("xs", [P, 2, KD, S])
        sq = st.sb("sq", [P, 2, 2, S])
        nn = st.sb("nn", [P, 2, 2, C])
        rn = st.sb("rn", [P, 2, 2, C])
        gate = st.sb("gate", [P, 2, S])
        q0 = st.sb("q0", [P, 2, S])
        q = st.sb("q", [P, 2, S])
        k = st.sb("k", [P, 2, S])
        tots = st.sb("tots", [P, 2, S])
        at = st.sb("at", [P, 2, C, P])
        v = st.sb("v", [P, 2, C, P])
        ktok = st.sb("ktok", [P, 2, C, P])
        state = st.sb("state", [P, 2, C - 1, P])
        oT = st.sb("oT", [P, 2, S])
        ps_p = [st.ps([P, S]) for x in range(2)]
        ps_l = [st.ps([P, C, P]) for x in range(2)]
        ps_kv = st.ps([P, C - 1, P])
        ps_o = st.ps([P, S])
        ps_y = [st.ps([P, 2, D]) for x in range(2)]
        c_in, ones_set, s_dve, s_pool = (st.sem(n) for n in ("c_in", "ones_set", "dve", "pool"))
        w_in = [st.sem(f"w_in{x}") for x in range(2)]
        xs_ready, p_full = st.sem("xs_ready"), st.sem("p_full")
        p_read = [st.sem(f"p_read{x}") for x in range(2)]
        nn_ready, root_ready, rn_ready = (st.sem(n) for n in ("nn_ready", "root_ready", "rn_ready"))
        tots_ready, v_ready = st.sem("tots_ready"), st.sem("v_ready")
        q_ready, l_full, l_read, k_up, kt_full = ([st.sem(f"{n}{x}") for x in range(2)] for n in (
            "q_ready", "l_full", "l_read", "k_up", "kt_full"))
        ktok_ready, kv_full, state_ready = st.sem("ktok_ready"), st.sem("kv_full"), st.sem("state_ready")
        o_full, oT_ready, y_full, y_added = (st.sem(n) for n in ("o_full", "oT_ready", "y_full", "y_added"))
        block = st.ctx.enter_context(nc.Block())
        masks_in = at[:, :, :, :].rearrange("p u c t -> p (u c) t")[:, 0:LEVELS, :]
        start = [0] + [S - (S >> x) for x in range(LEVELS)]

        def whole(u, level):
            n = S >> level
            t = gate[:, u, :] if level == 0 else tots[:, u, start[level]:start[level] + n]
            return t.rearrange("p (b two) -> p b two", two=2)

        def half(x, u, level, side):
            return x[:, u, :].rearrange("p (b two n) -> p b two n", two=2, n=1 << (level - 1))[:, :, side, :]

        def spread(u, level, side):
            n = 1 << (level - 1)
            return whole(u, level - 1)[:, :, 1 - side].unsqueeze(2).to_broadcast([P, S // (2 * n), n])

        @block.sync
        def _(sp):
            sp.dma_start(diag[:, :], a["c_ident"]).then_inc(c_in, 16)
            sp.dma_start(masks_in, a["c_masks"]).then_inc(c_in, 16)
            with sp.Fori(0, H // 2) as e:
                for x in range(2):
                    hd = e * 2 + x
                    sp.wait_ge(y_full, CREDIT + (hd - 1) * 2 * B)
                    sp.dma_start(w[:, x, :, :, :].rearrange("p a k n -> p (a k n)"),
                                 a["l1_w"][bass.ds(hd, 1), :, :].rearrange("o p n -> p (o n)")).then_inc(w_in[x], 16)
                    sp.dma_start(wo[:, x, :], a["l1_wo"][bass.ds(hd, 1), :, :].rearrange("o p n -> p (o n)"))\
                        .then_inc(w_in[x], 16)

        @block.gpsimd
        def _(pool):
            ch = Chain(pool, s_pool)
            for x in range(2):
                pool.sem_inc(k_up[x], CREDIT)
            with pool.Fori(0, H // 2) as e:
                for x in range(2):
                    with pool.Fori(0, NB) as i:
                        ch.restart()
                        m = (e * 2 + x) * NB + i
                        for u in range(2):
                            pool.wait_ge(p_full, CREDIT + m * JOBS - JOBS + 8)
                            pool.tensor_copy(xs[:, u, :, :], xnT[:, :, bass.ds((i * 2 + u) * S, S)])\
                                .then_inc(xs_ready, 1)
                        for level in range(1, LEVELS + 1):
                            for u in range(2):
                                if level == 2:
                                    pool.wait_ge(tots_ready, m * 2 + u + 1)
                                pool.wait_ge(l_full[u], CREDIT + m * (LEVELS + 1) + level + 1)
                                left = half(k, u, level, 0)
                                ins = pool.tensor_tensor(left, left, spread(u, level, 0), ALU.mult)
                                if level in CLEAN:
                                    ch.link(ins)
                                    ins = pool.tensor_scalar(left, left, TINY, TINY, ALU.add, ALU.subtract)
                                ins.then_inc(k_up[u], 1)

        @block.tensor
        def _(pe):
            for s in (p_full, *l_full, *kt_full, kv_full, o_full, y_full):
                pe.sem_inc(s, CREDIT)
            pe.wait_ge(ones_set, 1)
            with pe.Fori(0, H // 2) as e:
                for x in range(2):
                    with pe.Fori(0, NB) as i:
                        m = (e * 2 + x) * NB + i
                        pe.wait_ge(w_in[x], 32 * (e + 1))
                        for j in range(JOBS):
                            u, what = j // 4, j % 4 if j < 8 else 4
                            if j in (0, 4):
                                pe.wait_ge(xs_ready, m * 2 + u + 1)
                            pe.wait_ge(p_read[j % 2], CREDIT + m * (5 - j % 2) + j // 2)
                            if what < 3:
                                for kk in range(KD):
                                    ins = pe.matmul(ps_p[j % 2][:, :], w[:, x, what, kk, :], xs[:, u, kk, :],
                                                    start=kk == 0, stop=kk == KD - 1)
                            elif what == 3:
                                for c in range(C):
                                    for kk in range(KD):
                                        ins = pe.matmul(ps_p[j % 2][:, c * P:(c + 1) * P],
                                                        xs[:, u, kk, c * P:(c + 1) * P], w[:, x, 3, kk, :],
                                                        start=kk == 0, stop=kk == KD - 1)
                            else:
                                pe.wait_ge(p_read[1], CREDIT + (m + 1) * 4)
                                for n in range(4 * C):
                                    c = n % C
                                    ins = pe.matmul(ps_p[0][:, n:n + 1],
                                                    sq[:, n // (2 * C), n // C % 2, c * P:(c + 1) * P],
                                                    ones[:, 0:1], start=True, stop=True)
                            ins.then_inc(p_full, 1)
                        for level in range(LEVELS + 1):
                            for u in range(2):
                                if level == 0:
                                    pe.wait_ge(p_read[1], CREDIT + m * 4 + 2 * u + 1)
                                    pe.wait_ge(ktok_ready, CREDIT + m * 2 - 1 + u)
                                else:
                                    pe.wait_ge(l_read[u], CREDIT + m * (LEVELS + 1) + level)
                                if level == 1:
                                    pe.wait_ge(q_ready[u], m + 1)
                                if level > 1:
                                    pe.wait_ge(k_up[u], CREDIT + m * LEVELS + level - 1)
                                for c in range(C):
                                    ins = pe.matmul(ps_l[u][:, c, :], k[:, u, c * P:(c + 1) * P],
                                                    (q if level else q0)[:, u, c * P:(c + 1) * P],
                                                    start=True, stop=True)
                                ins.then_inc(l_full[u], 1)
                        for u in range(2):
                            pe.wait_ge(l_read[u], CREDIT + (m + 1) * (LEVELS + 1))
                            pe.wait_ge(k_up[u], CREDIT + (m + 1) * LEVELS)
                            for c in range(C):
                                ins = pe.transpose(ps_l[u][:, c, :], k[:, u, c * P:(c + 1) * P], ident[:, :])
                            ins.then_inc(kt_full[u], 1)
                        for u in range(2):
                            n = m * 2 + u
                            pe.wait_ge(v_ready, n + 1)
                            pe.wait_ge(ktok_ready, CREDIT + n + 1)
                            pe.wait_ge(state_ready, CREDIT + n)
                            for c in range(C - 1):
                                ins = pe.matmul(ps_kv[:, c, :], ktok[:, u, c, :], v[:, u, c, :],
                                                start=True, stop=True)
                            ins.then_inc(kv_full, 1)
                            pe.wait_ge(oT_ready, CREDIT + n)
                            pe.matmul(ps_o[:, 0:P], v[:, u, 0, :], at[:, u, 0, :], start=True, stop=True)
                            pe.wait_ge(state_ready, CREDIT + n + 1)
                            for c in range(1, C):
                                pe.matmul(ps_o[:, c * P:(c + 1) * P], v[:, u, c, :], at[:, u, c, :],
                                          start=True, stop=False)
                                ins = pe.matmul(ps_o[:, c * P:(c + 1) * P], state[:, u, c - 1, :],
                                                q[:, u, c * P:(c + 1) * P], start=False, stop=True)
                            ins.then_inc(o_full, 1)
                        for u in range(2):
                            n = m * 2 + u
                            pe.wait_ge(oT_ready, CREDIT + n + 1)
                            for y in range(2):
                                pe.wait_ge(y_added, CREDIT + n * 2 + y - 1)
                                for t in (2 * y, 2 * y + 1):
                                    ins = pe.matmul(ps_y[y][:, t % 2, :], oT[:, u, t * P:(t + 1) * P],
                                                    wo[:, x, :], start=True, stop=True)
                                ins.then_inc(y_full, 1)

        @block.scalar
        def _(act):
            for s in (ktok_ready, oT_ready):
                act.sem_inc(s, CREDIT)
            with act.Fori(0, H // 2) as e:
                for x in range(2):
                    with act.Fori(0, NB) as i:
                        m = (e * 2 + x) * NB + i
                        for j in range(8):
                            u, what = j // 4, j % 4
                            if what == 0:
                                act.wait_ge(y_added, CREDIT + (m - 1) * 4 + 2 * u + 2)
                                act.wait_ge(k_up[u], CREDIT + m * LEVELS)
                            act.wait_ge(p_full, CREDIT + m * JOBS + j + 1)
                            if what < 2:
                                act.activation((q0, k)[what][:, u, :], ps_p[j % 2][:, :], ACT.Copy, scale=UP)
                                ins = act.activation(sq[:, u, what, :], ps_p[j % 2][:, :], ACT.Square)
                            elif what == 2:
                                ins = act.activation(gate[:, u, :], ps_p[j % 2][:, :], ACT.Sigmoid)
                            else:
                                ins = act.activation(v[:, u, :, :], ps_p[j % 2][:, :].rearrange(
                                    "p (c n) -> p c n", c=C), ACT.Copy)
                            ins.then_inc(p_read[j % 2], 1)
                        act.wait_ge(nn_ready, m + 1)
                        act.activation(nn[:, :, :, :], nn[:, :, :, :], ACT.Sqrt).then_inc(root_ready, 1)
                        act.wait_ge(rn_ready, m + 1)
                        for u in range(2):
                            for c in range(C):
                                ins = act.activation(v[:, u, c, :], v[:, u, c, :], ACT.Copy,
                                                     scale=rn[:, u, 1, c:c + 1])
                            ins.then_inc(v_ready, 1)
                        for u in range(2):
                            act.wait_ge(kt_full[u], CREDIT + m + 1)
                            act.activation(ktok[:, u, :, :], ps_l[u][:, :, :], ACT.Copy).then_inc(ktok_ready, 1)
                        for u in range(2):
                            act.wait_ge(o_full, CREDIT + m * 2 + u + 1)
                            act.activation(oT[:, u, :], ps_o[:, :], ACT.Copy, scale=UP ** -2).then_inc(oT_ready, 1)

        @block.vector
        def _(dve):
            ch = Chain(dve, s_dve)
            dve.memset(ones[:, :], 1.0).then_inc(ones_set, 1)
            for s in (*p_read, *l_read, state_ready, y_added):
                dve.sem_inc(s, CREDIT)
            dve.wait_ge(c_in, 32)
            ch.link(dve.tensor_copy(masks[:, :, :], masks_in))
            with dve.Fori(0, H // 2) as e:
                for x in range(2):
                    with dve.Fori(0, NB) as i:
                        ch.restart()
                        m = (e * 2 + x) * NB + i
                        for u in range(2):
                            dve.wait_ge(p_read[0], CREDIT + m * 5 + 2 * u + 2)
                            ch.link(dve.tensor_tensor(q[:, u, :], q0[:, u, :], gate[:, u, :], ALU.mult))
                            dve.sem_inc(q_ready[u], 1)
                            for level in range(1, LEVELS + 1):
                                n = S >> level
                                o = start[level]
                                pair = whole(u, level - 1)
                                ch.link(dve.tensor_tensor(tots[:, u, o:o + n], pair[:, :, 0], pair[:, :, 1],
                                                          ALU.mult))
                            dve.sem_inc(tots_ready, 1)
                        dve.wait_ge(p_full, CREDIT + (m + 1) * JOBS)
                        ch.link(dve.tensor_scalar(nn[:, :, :, :].rearrange("p u w c -> p (u w c)"),
                                                  ps_p[0][:, 0:4 * C], EPS2, None, ALU.max))
                        dve.sem_inc(p_read[0], 1)
                        dve.sem_inc(nn_ready, 1)
                        for level in range(LEVELS + 1):
                            for u in range(2):
                                dve.wait_ge(l_full[u], CREDIT + m * (LEVELS + 1) + level + 1)
                                if level == 0:
                                    ch.link(dve.tensor_tensor(at[:, u, :, :], ps_l[u][:, :, :],
                                                              diag[:, :].unsqueeze(1).to_broadcast([P, C, P]),
                                                              ALU.mult))
                                else:
                                    right = half(q, u, level, 1)
                                    ins = dve.tensor_tensor(right, right, spread(u, level, 1), ALU.mult)
                                    if level in CLEAN:
                                        ch.link(ins)
                                        dve.tensor_scalar(right, right, TINY, TINY, ALU.add, ALU.subtract)
                                    ch.link(dve.copy_predicated(
                                        at[:, u, :, :],
                                        masks[:, level - 1, :].unsqueeze(1).to_broadcast([P, C, P]),
                                        ps_l[u][:, :, :]))
                                dve.sem_inc(l_read[u], 1)
                            if level == 0:
                                dve.wait_ge(root_ready, m + 1)
                                ch.link(dve.reciprocal(rn[:, :, :, :], nn[:, :, :, :]))
                                dve.sem_inc(rn_ready, 1)
                        for u in range(2):
                            n = m * 2 + u
                            dve.wait_ge(kv_full, CREDIT + n + 1)
                            ch.link(dve.tensor_copy(state[:, u, 0, :], ps_kv[:, 0, :]))
                            last = start[LEVELS]
                            for c in range(1, C - 1):
                                ch.link(dve.scalar_tensor_tensor(
                                    out=state[:, u, c, :], in0=state[:, u, c - 1, :],
                                    scalar=tots[:, u, last + c:last + c + 1], in1=ps_kv[:, c, :],
                                    op0=ALU.mult, op1=ALU.add))
                            dve.sem_inc(state_ready, 1)
                        for u in range(2):
                            n = m * 2 + u
                            for y in range(2):
                                dve.wait_ge(y_full, CREDIT + n * 2 + y + 1)
                                for t in (2 * y, 2 * y + 1):
                                    tile = h[:, (i * 2 + u) * TPB + t, :]
                                    ins = dve.scalar_tensor_tensor(out=tile, in0=ps_y[y][:, t % 2, :],
                                                                   scalar=rn[:, u, 0, t:t + 1], in1=tile,
                                                                   op0=ALU.mult, op1=ALU.add)
                                ins.then_inc(y_added, 1)


def l1_ffn_stage(nc, h, xnT, a):
    M, UN = 64, 8
    with Stage(nc, "l1f") as st:
        win = st.sb("win", [P, KD, P])
        wout = st.sb("wout", [P, D])
        bout = st.sb("bout", [P, D])
        cols = st.sb("cols", [P, 3 * UN + 2])
        w1, b1, w2 = (cols[:, k * UN:(k + 1) * UN] for k in range(3))
        s_sb = st.sb("s", [P, 2, S])
        unit = st.sb("unit", [P, 2, UN, S])
        acc = st.sb("acc", [P, 2, S])
        ps_s = [st.ps([P, S]) for k in range(2)]
        ps_y = [st.ps([P, 2, D]) for k in range(2)]
        w_in, s_dve, s_act = st.sem("w_in"), st.sem("dve"), st.sem("act")
        bias_added, s_full, unit_ready = st.sem("bias_added"), st.sem("s_full"), st.sem("unit_ready")
        acc_ready, y_full, y_added = st.sem("acc_ready"), st.sem("y_full"), st.sem("y_added")
        block = st.ctx.enter_context(nc.Block())

        @block.sync
        def _(sp):
            for dst, src in ((win[:, :, :], a["win"]), (wout[:, :], a["wout"]), (bout[:, :], a["bout"]),
                             (cols[:, :], a["l1f_cols"])):
                sp.dma_start(dst, src).then_inc(w_in, 16)

        @block.gpsimd
        def _(pool):
            pool.wait_ge(w_in, 4 * 16)
            with pool.Fori(0, TILES) as n:
                pool.tensor_tensor(h[:, n, :], h[:, n, :], bout[:, :], ALU.add).then_inc(bias_added, 1)

        @block.tensor
        def _(pe):
            for s in (s_full, y_full):
                pe.sem_inc(s, CREDIT)
            pe.wait_ge(w_in, 4 * 16)

            def channels(b, u):
                pe.wait_ge(unit_ready, CREDIT + (b - 1) * UN)
                for k in range(KD):
                    ins = pe.matmul(ps_s[u][:, :], win[:, k, :], xnT[:, k, bass.ds(b * S, S)],
                                    start=k == 0, stop=k == KD - 1)
                ins.then_inc(s_full, 1)

            with pe.Fori(0, B // 2) as i:
                for u in range(2):
                    channels(i * 2 + u, u)
                for u in range(2):
                    b = i * 2 + u
                    pe.wait_ge(acc_ready, CREDIT + b + 1)
                    for y in range(2):
                        pe.wait_ge(y_added, CREDIT + b * 2 + y - 1)
                        for t in (2 * y, 2 * y + 1):
                            ins = pe.matmul(ps_y[y][:, t % 2, :], acc[:, u, t * P:(t + 1) * P], wout[:, :],
                                            start=True, stop=True)
                        ins.then_inc(y_full, 1)

        @block.scalar
        def _(act):
            ch = Chain(act, s_act)
            act.sem_inc(unit_ready, CREDIT)
            act.wait_ge(w_in, 4 * 16)
            with act.Fori(0, B // 2) as i:
                ch.restart()
                for u in range(2):
                    b = i * 2 + u
                    act.wait_ge(s_full, CREDIT + b + 1)
                    ch.link(act.activation(s_sb[:, u, :], ps_s[u][:, :], ACT.Identity,
                                           bias=cols[:, 3 * UN:3 * UN + 1]))
                    act.wait_ge(acc_ready, CREDIT + b - 1)
                    for k in range(UN):
                        act.activation(unit[:, u, k, :], s_sb[:, u, :], ACT.Relu, scale=w1[:, k:k + 1],
                                       bias=b1[:, k:k + 1]).then_inc(unit_ready, 1)

        @block.vector
        def _(dve):
            ch = Chain(dve, s_dve)
            dve.sem_inc(y_added, CREDIT)
            dve.sem_inc(acc_ready, CREDIT)
            dve.wait_ge(w_in, 4 * 16)
            with dve.Fori(0, B // 2) as i:
                ch.restart()
                for u in range(2):
                    b = i * 2 + u
                    dve.wait_ge(y_full, CREDIT + (b - 1) * 2)
                    for k in range(UN):
                        dve.wait_ge(unit_ready, CREDIT + b * UN + k + 1)
                        if k == 0:
                            ch.link(dve.tensor_scalar(acc[:, u, :], unit[:, u, 0, :], w2[:, 0:1],
                                                      cols[:, 3 * UN + 1:3 * UN + 2], ALU.mult, ALU.add))
                        else:
                            ch.link(dve.scalar_tensor_tensor(out=acc[:, u, :], in0=unit[:, u, k, :],
                                                             scalar=w2[:, k:k + 1], in1=acc[:, u, :],
                                                             op0=ALU.mult, op1=ALU.add))
                    dve.sem_inc(acc_ready, 1)
                for u in range(2):
                    b = i * 2 + u
                    dve.wait_ge(bias_added, (b + 1) * TPB)
                    for y in range(2):
                        dve.wait_ge(y_full, CREDIT + b * 2 + y + 1)
                        two = h[:, bass.ds(b * TPB + 2 * y, 2), :]
                        dve.tensor_tensor(two, two, ps_y[y][:, :, :], ALU.add).then_inc(y_added, 1)


def l2_attn_stage(nc, h, xnT, ident, a):
    HG, HD, G = 2, 16, 8
    R = S // P
    SCALE = HD ** -0.5
    VW = P + HD
    JOBS = 6
    NH = HG * G
    NEG = -1e30
    with Stage(nc, "l2a") as st:
        wq, wk, wv, wo = (st.sb(n, [P, KD, D]) for n in ("wq", "wk", "wv", "wo"))
        cols = st.sb("cols", [P, G])
        future = st.sb("future", [P, P])
        xs = st.sb("xs", [P, KD, S])
        qT = st.sb("qT", [P, HG, S])
        kT = st.sb("kT", [P, HG, G, S])
        v = st.sb("v", [P, R, HG, G * VW])
        p = st.sb("p", [P, 2, R, S])
        pT = st.sb("pT", [P, 2, R, S])
        oT = st.sb("oT", [P, HG, S])
        nmx = st.sb("nmx", [P, 2, R])
        sums = st.sb("sums", [P, 2, R])
        rsum = st.sb("rsum", [P, 2, R])
        ps_s = [st.ps([P, S]) for x in range(3)]
        ps_t = [st.ps([P, S]) for x in range(2)]
        ps_o = st.ps([P, S])
        ps_p = [st.ps([P, S]) for x in range(2)]
        w_in, s_dve, v_zero, xs_ready, p_full = (st.sem(n) for n in ("w_in", "dve", "v_zero", "xs_ready", "p_full"))
        p_read = [st.sem(f"p_read{x}") for x in range(2)]
        s_full = st.sem("s_full")
        nmx_ready, exp_done, p_ready, t_full = (st.sem(n) for n in ("nmx_ready", "exp_done", "p_ready", "t_full"))
        pT_ready = [st.sem(f"pT_ready{x}") for x in range(2)]
        o_full, oT_ready, y_full = (st.sem(n) for n in ("o_full", "oT_ready", "y_full"))
        y_added = st.sem("y_added")
        block = st.ctx.enter_context(nc.Block())

        @block.sync
        def _(sp):
            for dst, src in ((wq[:, :, :], a["wq2"]), (wk[:, :, :], a["wk2"]), (wv[:, :, :], a["wv2"]),
                             (wo[:, :, :], a["wo2"]), (cols[:, :], a["c_heads"]), (future[:, :], a["c_future"])):
                sp.dma_start(dst, src).then_inc(w_in, 16)

        @block.gpsimd
        def _(pool):
            pool.memset(v[:, :, :, :], 0.0).then_inc(v_zero, 1)
            with pool.Fori(0, B) as b:
                pool.wait_ge(p_full, CREDIT + (b - 1) * JOBS + JOBS)
                pool.tensor_copy(xs[:, :, :], xnT[:, :, bass.ds(b * S, S)]).then_inc(xs_ready, 1)

        @block.tensor
        def _(pe):
            for s in (p_full, t_full, o_full, y_full, s_full):
                pe.sem_inc(s, CREDIT)
            pe.wait_ge(w_in, 6 * 16)
            with pe.Fori(0, B) as b:
                pe.wait_ge(xs_ready, b + 1)
                pe.wait_ge(y_added, CREDIT + b * 2)
                for j in range(JOBS):
                    pe.wait_ge(p_read[j % 2], CREDIT + b * JOBS // 2 + j // 2)
                    for x in range(1 if j < 4 else 2):
                        for k in range(KD):
                            if j < 4:
                                ins = pe.matmul(ps_p[j % 2][:, :], (wq, wk)[j // 2][:, k, (j % 2) * P:(j % 2 + 1) * P],
                                                xs[:, k, :], start=k == 0, stop=k == KD - 1)
                            else:
                                t = 2 * (j - 4) + x
                                ins = pe.matmul(ps_p[j % 2][:, x * D:(x + 1) * D], xs[:, k, t * P:(t + 1) * P],
                                                wv[:, k, :], start=k == 0, stop=k == KD - 1)
                    ins.then_inc(p_full, 1)

                def scores(hh):
                    for r in range(R):
                        s = (hh * R + r) % 3
                        pe.wait_ge(exp_done, CREDIT + (b * NH + hh) * R + r - 2)
                        pe.matmul(ps_s[s][:, 0:(r + 1) * P], qT[:, hh // G, r * P:(r + 1) * P],
                                  kT[:, hh // G, hh % G, 0:(r + 1) * P], start=True, stop=True).then_inc(s_full, 1)

                for x in range(2):
                    pe.wait_ge(p_read[x], CREDIT + (b + 1) * JOBS // 2)
                scores(0)
                for hh in range(NH):
                    g = hh // G
                    if hh + 1 < NH:
                        scores(hh + 1)
                    pe.wait_ge(p_ready, b * NH + hh + 1)
                    for kt in range(R):
                        pe.wait_ge(pT_ready[kt % 2], CREDIT + (b * NH + hh) * 2 + kt // 2)
                        for r in range(kt, R):
                            ins = pe.transpose(ps_t[kt % 2][:, r * P:(r + 1) * P],
                                               p[:, hh % 2, r, kt * P:(kt + 1) * P], ident[:, :])
                        ins.then_inc(t_full, 1)
                    if hh % G == 0:
                        pe.wait_ge(oT_ready, CREDIT + b * HG + g)
                    for kt in range(R):
                        pe.wait_ge(pT_ready[kt % 2], CREDIT + (b * NH + hh) * 2 + kt // 2 + 1)
                        ins = pe.matmul(ps_o[:, kt * P:], v[:, kt, g, (hh % G) * P:(hh % G + 1) * P],
                                        pT[:, hh % 2, kt, kt * P:], start=hh % G == 0 and kt == 0,
                                        stop=hh % G == G - 1 and kt == R - 1, skip_group_check=True)
                    ins.then_inc(o_full, 1)
                pe.wait_ge(oT_ready, CREDIT + (b + 1) * HG)
                for y in range(2):
                    for t in (2 * y, 2 * y + 1):
                        for g in range(HG):
                            ins = pe.matmul(ps_p[y][:, (t % 2) * D:(t % 2 + 1) * D], oT[:, g, t * P:(t + 1) * P],
                                            wo[:, g, :], start=g == 0, stop=g == HG - 1)
                    ins.then_inc(y_full, 1)

        @block.scalar
        def _(act):
            for s in (exp_done, oT_ready, pT_ready[1]):
                act.sem_inc(s, CREDIT)
            act.wait_ge(w_in, 6 * 16)
            with act.Fori(0, B) as b:
                act.wait_ge(s_full, CREDIT + b * NH * R)
                for j in range(4):
                    act.wait_ge(p_full, CREDIT + b * JOBS + j + 1)
                    if j < 2:
                        ins = act.activation(qT[:, j, :], ps_p[j % 2][:, :], ACT.Copy, scale=SCALE)
                    else:
                        for g in range(G):
                            ins = act.activation(kT[:, j % 2, g, :], ps_p[j % 2][:, :], ACT.Copy,
                                                 scale=cols[:, g:g + 1])
                    ins.then_inc(p_read[j % 2], 1)

                def exps(hh, rows):
                    act.wait_ge(t_full, CREDIT + (b * NH + hh - 1) * R)
                    for r in rows:
                        act.wait_ge(nmx_ready, (b * NH + hh) * R + r + 1)
                        act.activation(p[:, hh % 2, r, 0:(r + 1) * P], ps_s[(hh * R + r) % 3][:, 0:(r + 1) * P],
                                       ACT.Exp, bias=nmx[:, hh % 2, r:r + 1],
                                       accum_out=sums[:, hh % 2, r:r + 1]).then_inc(exp_done, 1)

                exps(0, range(R))
                for hh in range(NH):
                    for kt in (1, 3):
                        if hh + 1 < NH:
                            exps(hh + 1, (0, 1) if kt == 1 else (2,))
                        act.wait_ge(t_full, CREDIT + (b * NH + hh) * R + kt + 1)
                        act.wait_ge(o_full, CREDIT + b * NH + hh - 1)
                        act.activation(pT[:, hh % 2, kt, kt * P:], ps_t[1][:, kt * P:], ACT.Copy)\
                            .then_inc(pT_ready[1], 1)
                    if hh + 1 < NH:
                        exps(hh + 1, (3,))
                    if hh % G == G - 1:
                        act.wait_ge(o_full, CREDIT + b * NH + hh + 1)
                        act.wait_ge(y_full, CREDIT + b * 2)
                        act.activation(oT[:, hh // G, :], ps_o[:, :], ACT.Copy).then_inc(oT_ready, 1)

        @block.vector
        def _(dve):
            ch = Chain(dve, s_dve)
            for s in (*p_read, pT_ready[0], y_added):
                dve.sem_inc(s, CREDIT)
            dve.wait_ge(w_in, 6 * 16)
            dve.wait_ge(v_zero, 1)
            with dve.Fori(0, B) as b:
                ch.restart()
                for j in (4, 5):
                    dve.wait_ge(o_full, CREDIT + b * NH)
                    dve.wait_ge(p_full, CREDIT + b * JOBS + j + 1)
                    for x in range(2):
                        dst = v[:, 2 * (j - 4) + x, :, :].rearrange("p m (g w) -> p m g w", w=VW)[:, :, :, 0:HD]
                        ins = dve.tensor_copy(dst, ps_p[j % 2][:, x * D:(x + 1) * D].rearrange(
                            "p (m g w) -> p m g w", m=HG, w=HD))
                    ins.then_inc(p_read[j % 2], 1)

                def maxima(hh, rows):
                    dve.wait_ge(exp_done, CREDIT + (b * NH + hh - 1) * R)
                    for r in rows:
                        s = ps_s[(hh * R + r) % 3]
                        dve.wait_ge(s_full, CREDIT + (b * NH + hh) * R + r + 1)
                        ch.link(dve.tensor_tensor(s[:, r * P:(r + 1) * P], s[:, r * P:(r + 1) * P],
                                                  future[:, :], ALU.add))
                        dve.tensor_reduce(nmx[:, hh % 2, r:r + 1], s[:, 0:(r + 1) * P], X, ALU.max,
                                          negate=True).then_inc(nmx_ready, 1)

                maxima(0, range(R))
                for hh in range(NH):
                    if hh + 1 < NH:
                        maxima(hh + 1, (0,))
                    dve.wait_ge(exp_done, CREDIT + (b * NH + hh + 1) * R)
                    ch.link(dve.reciprocal(rsum[:, hh % 2, :], sums[:, hh % 2, :]))
                    for r in range(R):
                        ins = dve.tensor_scalar(p[:, hh % 2, r, 0:(r + 1) * P], p[:, hh % 2, r, 0:(r + 1) * P],
                                                rsum[:, hh % 2, r:r + 1], None, ALU.mult)
                    ins.then_inc(p_ready, 1)
                    for kt in (0, 2):
                        if hh + 1 < NH:
                            maxima(hh + 1, (1 + kt // 2,))
                        dve.wait_ge(t_full, CREDIT + (b * NH + hh) * R + kt + 1)
                        dve.wait_ge(o_full, CREDIT + b * NH + hh - 1)
                        dve.tensor_copy(pT[:, hh % 2, kt, kt * P:], ps_t[0][:, kt * P:]).then_inc(pT_ready[0], 1)
                    if hh + 1 < NH:
                        maxima(hh + 1, (3,))
                for y in range(2):
                    dve.wait_ge(y_full, CREDIT + b * 2 + y + 1)
                    two = h[:, bass.ds(b * TPB + 2 * y, 2), :]
                    dve.tensor_tensor(two, two, ps_p[y][:, :].rearrange("p (t d) -> p t d", t=2), ALU.add)\
                        .then_inc(y_added, 1)


EXPERTS, F = 8, 1024
KF = F // P
WE = EXPERTS + 1


def routing_stage(nc, h, xnT, ident, a, gates):
    CAP = max(int(1.25 * (B * S * 2 / EXPERTS)), 4)
    with Stage(nc, "rt") as st:
        wr = st.sb("wr", [P, KD, EXPERTS])
        b2 = st.sb("b2", [WE, D])
        upto = st.sb("upto", [P, P])
        ones = st.sb("ones", [P, P])
        rank = st.sb("rank", [P, EXPERTS])
        xs = st.sb("xs", [P, 2, KD, P])
        full = lambda name: st.sb(name, [P, TILES, EXPERTS])
        few = lambda name: st.sb(name, [P, TILES])
        pr, one, two, hit, w, t1 = (full(n) for n in ("pr", "one", "two", "hit", "w", "t1"))
        mx, sm, m1, m2, best, ns = (few(n) for n in ("mx", "sm", "m1", "m2", "best", "ns"))
        elig, cum, place, kept, alive, zero = (few(n) for n in ("elig", "cum", "place", "kept", "alive", "zero"))
        gT = st.sb("gT", [WE, 2, 4, P])
        ps_l = st.ps([P, TILES, EXPERTS])
        ps_c = [st.ps([P, TILES]) for x in range(2)]
        ps_g = [st.ps([WE, 4, P]) for x in range(2)]
        ps_y = [st.ps([P, 2, D]) for x in range(2)]
        w_in, s_dve, xs_ready, l_full = (st.sem(n) for n in ("w_in", "dve", "xs_ready", "l_full"))
        ready, exp_done, elig_ready, c_full = (st.sem(n) for n in ("ready", "exp_done", "elig_ready", "c_full"))
        gates_ready, g_full, gT_ready, y_full, y_added = (st.sem(n) for n in (
            "gates_ready", "g_full", "gT_ready", "y_full", "y_added"))
        block = st.ctx.enter_context(nc.Block())

        @block.sync
        def _(sp):
            for dst, src in ((wr[:, :, :], a["wr"]), (b2[:, :], a["moe_b2"]), (upto[:, :], a["c_upto"]),
                             (rank[:, :], a["c_rank8"])):
                sp.dma_start(dst, src).then_inc(w_in, 16)

        @block.gpsimd
        def _(pool):
            with pool.Fori(0, TILES // 2) as i:
                for u in range(2):
                    n = i * 2 + u
                    pool.wait_ge(l_full, CREDIT + n - 1)
                    pool.tensor_copy(xs[:, u, :, :], xnT[:, :, bass.ds(n * P, P)]).then_inc(xs_ready, 1)

        @block.tensor
        def _(pe):
            pe.sem_inc(l_full, CREDIT)
            pe.wait_ge(w_in, 4 * 16)
            with pe.Fori(0, TILES // 2) as i:
                for u in range(2):
                    n = i * 2 + u
                    pe.wait_ge(xs_ready, n + 1)
                    for k in range(KD):
                        ins = pe.matmul(ps_l[:, bass.ds(n, 1), :], xs[:, u, k, :], wr[:, k, :],
                                        start=k == 0, stop=k == KD - 1)
                    ins.then_inc(l_full, 1)
            for e in range(EXPERTS):
                pe.wait_ge(elig_ready, e + 1)
                pe.matmul(ps_c[0][:, :], upto[:, :], elig[:, :], start=True, stop=True)
                pe.matmul(ps_c[1][:, :], ones[:, :], elig[:, :], start=True, stop=True).then_inc(c_full, 1)
            pe.wait_ge(gates_ready, 1)
            for q in range(TILES // 4):
                if q >= 2:
                    pe.wait_ge(gT_ready, q - 1)
                for t in range(4):
                    ins = pe.transpose(ps_g[q % 2][:, t, :], gates[:, 4 * q + t, :], ident[:, :])
                ins.then_inc(g_full, 1)
                pe.wait_ge(gT_ready, q + 1)
                for y in range(2):
                    if q:
                        pe.wait_ge(y_added, 2 * q - 1 + y)
                    for t in range(2):
                        ins = pe.matmul(ps_y[y][:, t, :], gT[:, q % 2, 2 * y + t, :], b2[:, :],
                                        start=True, stop=True)
                    ins.then_inc(y_full, 1)

        @block.scalar
        def _(act):
            act.wait_ge(ready, 1)
            act.activation(pr[:, :, :], t1[:, :, :], ACT.Exp).then_inc(exp_done, 1)
            for q in range(TILES // 4):
                act.wait_ge(g_full, q + 1)
                if q >= 2:
                    act.wait_ge(y_full, 2 * (q - 1))
                act.activation(gT[:, q % 2, :, :], ps_g[q % 2][:, :, :], ACT.Copy).then_inc(gT_ready, 1)

        @block.vector
        def _(dve):
            ch = Chain(dve, s_dve)
            wide = lambda x: x[:, :].unsqueeze(2).to_broadcast([P, TILES, EXPERTS])
            ranks = rank[:, :].unsqueeze(1).to_broadcast([P, TILES, EXPERTS])
            ch.link(dve.memset(zero[:, :], 0.0))
            ch.link(dve.memset(ones[:, :], 1.0))
            ch.link(dve.memset(alive[:, :], 1.0))
            dve.wait_ge(w_in, 4 * 16)
            dve.wait_ge(l_full, CREDIT + TILES)
            ch.link(dve.tensor_reduce(mx[:, :], ps_l[:, :, :], X, ALU.max))
            ch.link(dve.tensor_tensor(t1[:, :, :], ps_l[:, :, :], wide(mx), ALU.subtract))
            dve.sem_inc(ready, 1)
            dve.wait_ge(exp_done, 1)
            ch.link(dve.tensor_reduce(sm[:, :], pr[:, :, :], X, ALU.add))
            ch.link(dve.reciprocal(sm[:, :], sm[:, :]))
            ch.link(dve.tensor_tensor(pr[:, :, :], pr[:, :, :], wide(sm), ALU.mult))

            def first_largest(hot, m):
                ch.link(dve.tensor_reduce(m[:, :], pr[:, :, :], X, ALU.max))
                ch.link(dve.tensor_tensor(t1[:, :, :], pr[:, :, :], wide(m), ALU.is_ge))
                ch.link(dve.tensor_tensor(t1[:, :, :], t1[:, :, :], ranks, ALU.mult))
                ch.link(dve.tensor_reduce(best[:, :], t1[:, :, :], X, ALU.max))
                ch.link(dve.tensor_tensor(hot[:, :, :], t1[:, :, :], wide(best), ALU.is_equal))

            first_largest(one, m1)
            ch.link(dve.scalar_tensor_tensor(out=pr[:, :, :], in0=one[:, :, :], scalar=-2.0, in1=pr[:, :, :],
                                             op0=ALU.mult, op1=ALU.add))
            first_largest(two, m2)
            ch.link(dve.tensor_tensor(hit[:, :, :], one[:, :, :], two[:, :, :], ALU.add))
            ch.link(dve.tensor_tensor(ns[:, :], m1[:, :], m2[:, :], ALU.add))
            ch.link(dve.tensor_scalar(ns[:, :], ns[:, :], 1e-9, None, ALU.max))
            ch.link(dve.reciprocal(ns[:, :], ns[:, :]))
            for hot, m in ((one, m1), (two, m2)):
                ch.link(dve.tensor_tensor(m[:, :], m[:, :], ns[:, :], ALU.mult))
                ch.link(dve.tensor_tensor(hot[:, :, :], hot[:, :, :], wide(m), ALU.mult))
            ch.link(dve.tensor_tensor(w[:, :, :], one[:, :, :], two[:, :, :], ALU.add))
            for e in range(EXPERTS):
                dve.tensor_tensor(elig[:, :], hit[:, :, e], alive[:, :], ALU.mult).then_inc(elig_ready, 1)
                dve.wait_ge(c_full, e + 1)
                ch.link(dve.tensor_tensor_scan(cum[:, :], ps_c[1][:, :], zero[:, :], 0.0, ALU.add, ALU.add))
                ch.link(dve.tensor_tensor(place[:, :], cum[:, :], ps_c[1][:, :], ALU.subtract))
                ch.link(dve.tensor_tensor(place[:, :], place[:, :], ps_c[0][:, :], ALU.add))
                ch.link(dve.scalar_tensor_tensor(out=kept[:, :], in0=place[:, :], scalar=float(CAP),
                                                 in1=elig[:, :], op0=ALU.is_le, op1=ALU.mult))
                ch.link(dve.tensor_tensor(gates[:, :, e], w[:, :, e], kept[:, :], ALU.mult))
                ch.link(dve.tensor_tensor(place[:, :], elig[:, :], kept[:, :], ALU.subtract))
                ch.link(dve.tensor_tensor(alive[:, :], alive[:, :], place[:, :], ALU.subtract))
            ch.link(dve.tensor_tensor(gates[:, :, 0:EXPERTS], gates[:, :, 0:EXPERTS], wide(alive), ALU.mult))
            dve.tensor_scalar(gates[:, :, EXPERTS], alive[:, :], -1.0, 1.0, ALU.mult, ALU.add)\
                .then_inc(gates_ready, 1)
            for q in range(TILES // 4):
                for y in range(2):
                    dve.wait_ge(y_full, 2 * q + y + 1)
                    pair = h[:, 4 * q + 2 * y:4 * q + 2 * y + 2, :]
                    dve.tensor_tensor(pair, pair, ps_y[y][:, :, :], ALU.add).then_inc(y_added, 1)


def ffn_stage(nc, name, h, xnT, experts, load, gates=None, w1=None, w2=None, b1=None, bias=None):
    NB = B // 2
    single = experts == 1
    with Stage(nc, name) as st:
        if not single:
            w1 = st.sb("w1", [P, 2, KD, F])
            w2 = st.sb("w2", [P, 2, KF, D])
            b1 = st.sb("b1", [P, 2, KF])
        mid = st.sb("mid", [P, 2, KF, S])
        ps_m = [st.ps([P, S]) for x in range(4)]
        ps_y = [st.ps([P, 2, D]) for x in range(4)]
        m_full, mid_ready, y_full, y_added, bias_added = (st.sem(n) for n in (
            "m_full", "mid_ready", "y_full", "y_added", "bias_added"))
        w_in = [st.sem(f"w_in{x}") for x in range(2)]
        block = st.ctx.enter_context(nc.Block())

        def experts_loop(eng, body):
            if experts > 1:
                with eng.Fori(0, experts // 2) as ep:
                    for x in range(2):
                        with eng.Fori(0, NB) as i:
                            body(ep * 2 + x, x, i, ep + 1)
            with eng.Fori(0, NB) as i:
                body(experts - 1, 0, i, experts // 2 + 1)

        @block.sync
        def _(sp):
            if not single:
                with sp.Fori(0, experts // 2) as ep:
                    for x in range(2):
                        e = ep * 2 + x
                        sp.wait_ge(y_full, CREDIT + (e - 1) * 2 * B)
                        load(sp, e, w1[:, x, :, :], w2[:, x, :, :], b1[:, x, :], w_in[x])
                sp.wait_ge(y_full, CREDIT + (experts - 2) * 2 * B)
                load(sp, experts - 1, w1[:, 0, :, :], w2[:, 0, :, :], b1[:, 0, :], w_in[0])

        @block.gpsimd
        def _(pool):
            if single:
                with pool.Fori(0, TILES) as n:
                    pool.tensor_tensor(h[:, n, :], h[:, n, :], bias, ALU.add).then_inc(bias_added, 1)

        @block.tensor
        def _(pe):
            for s in (m_full, y_full):
                pe.sem_inc(s, CREDIT)

            def body(e, x, i, loads):
                m = e * NB + i
                if not single:
                    pe.wait_ge(w_in[x], 48 * loads)
                for u in range(2):
                    n = m * 2 + u
                    for f in range(KF):
                        pe.wait_ge(mid_ready, CREDIT + n * KF + f - 3)
                        for k in range(KD):
                            ins = pe.matmul(ps_m[f % 4][:, :], w1[:, x, k, f * P:(f + 1) * P],
                                            xnT[:, k, bass.ds((i * 2 + u) * S, S)],
                                            start=k == 0, stop=k == KD - 1)
                        ins.then_inc(m_full, 1)
                for u in range(2):
                    n = m * 2 + u
                    pe.wait_ge(mid_ready, CREDIT + (n + 1) * KF)
                    for y in range(2):
                        pe.wait_ge(y_added, CREDIT + n * 2 + y - 3)
                        for t in range(2):
                            for f in range(KF):
                                c = (2 * y + t) * P
                                ins = pe.matmul(ps_y[2 * u + y][:, t, :], mid[:, u, f, c:c + P], w2[:, x, f, :],
                                                start=f == 0, stop=f == KF - 1)
                        ins.then_inc(y_full, 1)

            experts_loop(pe, body)

        @block.scalar
        def _(act):
            act.sem_inc(mid_ready, CREDIT)

            def body(e, x, i, loads):
                for u in range(2):
                    n = (e * NB + i) * 2 + u
                    act.wait_ge(y_full, CREDIT + (n - 1) * 2)
                    for f in range(KF):
                        act.wait_ge(m_full, CREDIT + n * KF + f + 1)
                        act.activation(mid[:, u, f, :], ps_m[f % 4][:, :], ACT.Gelu, bias=b1[:, x, f:f + 1])\
                            .then_inc(mid_ready, 1)

            experts_loop(act, body)

        @block.vector
        def _(dve):
            dve.sem_inc(y_added, CREDIT)
            if single:
                dve.wait_ge(bias_added, TILES)

            def body(e, x, i, loads):
                for u in range(2):
                    n = (e * NB + i) * 2 + u
                    for y in range(2):
                        dve.wait_ge(y_full, CREDIT + n * 2 + y + 1)
                        tile = (i * 2 + u) * TPB + 2 * y
                        if single:
                            two = h[:, bass.ds(tile, 2), :]
                            dve.tensor_tensor(two, two, ps_y[2 * u + y][:, :, :], ALU.add).then_inc(y_added, 1)
                            continue
                        for t in range(2):
                            flat = gates[:, :, :].rearrange("p t e -> p (t e)")
                            ins = dve.scalar_tensor_tensor(
                                out=h[:, tile + t, :], in0=ps_y[2 * u + y][:, t, :],
                                scalar=flat[:, bass.ds((tile + t) * WE + e, 1)], in1=h[:, tile + t, :],
                                op0=ALU.mult, op1=ALU.add)
                        ins.then_inc(y_added, 1)

            experts_loop(dve, body)


def l3_attn_stage(nc, h, xnT, ident, a):
    HG, G, HD, NFT = 2, 8, 16, 64
    NH = HG * G
    VA = HD + 1
    PAIRS = NH // 2
    W2 = 2 * VA
    JOBS = 6 + 2 * TPB * HG
    NORM = HD ** -0.25
    with Stage(nc, "l3a") as st:
        wq, wk, wv, wo = (st.sb(n, [P, KD, D]) for n in ("wq", "wk", "wv", "wo"))
        pm = st.sb("pm", [P, G * NFT])
        own = st.sb("own", [P, W2])
        cols = st.sb("cols", [P, 5])
        bv, bo = st.sb("bv", [P, D]), st.sb("bo", [P, D])
        xs = st.sb("xs", [P, KD, S])
        qk = st.sb("qk", [P, 2, HG, S])
        v = st.sb("v", [P, TPB, NH, VA])
        top = st.sb("top", [P, 2, G])
        shifted = st.sb("shifted", [P, 2, G * NFT])
        kf = st.sb("kf", [P, TPB, NH * NFT])
        qf = st.sb("qf", [P, 2, NH * NFT])
        qfT = st.sb("qfT", [P, 2, PAIRS, P])
        kv = st.sb("kv", [P, PAIRS, W2])
        den = st.sb("den", [P, 2, NH])
        o = st.sb("o", [P, 2, D])
        oT = st.sb("oT", [P, 2, KD, P])
        ps_p = [st.ps([P, S]) for x in range(2)]
        ps_kv = st.ps([P, PAIRS, W2])
        ps_t = [st.ps([P, 4, P]) for x in range(2)]
        ps_o = st.ps([P, PAIRS, W2])
        ps_ot = st.ps([P, KD, P])
        ps_y = st.ps([P, D])
        w_in, s_dve, ones_set, xs_ready, p_full = (st.sem(n) for n in ("w_in", "dve", "ones_set", "xs_ready", "p_full"))
        p_read = [st.sem(f"p_read{x}") for x in range(2)]
        shift_ready, feat_ready, kv_full, kv_ready = (st.sem(n) for n in ("shift_ready", "feat_ready", "kv_full", "kv_ready"))
        t_full, qfT_ready, o_full, o_ready = (st.sem(n) for n in ("t_full", "qfT_ready", "o_full", "o_ready"))
        ot_full, oT_ready, y_full, y_added = (st.sem(n) for n in ("ot_full", "oT_ready", "y_full", "y_added"))
        block = st.ctx.enter_context(nc.Block())
        NW = 9
        NFE = 2 * TPB * HG

        @block.sync
        def _(sp):
            for dst, src in ((wq[:, :, :], a["wq3"]), (wk[:, :, :], a["wk3"]), (wv[:, :, :], a["wv3"]),
                             (wo[:, :, :], a["wo3"]), (pm[:, :], a["pm3"]), (own[:, :], a["c_own"]),
                             (cols[:, :], a["l3a_cols"]), (bv[:, :], a["bv3"]), (bo[:, :], a["bo3"])):
                sp.dma_start(dst, src).then_inc(w_in, 16)

        @block.gpsimd
        def _(pool):
            pool.wait_ge(w_in, NW * 16)
            with pool.Fori(0, B) as b:
                for t in range(TPB):
                    pool.tensor_tensor(h[:, b * TPB + t, :], h[:, b * TPB + t, :], bo[:, :], ALU.add)
                pool.wait_ge(p_full, CREDIT + b * JOBS)
                pool.tensor_copy(xs[:, :, :], xnT[:, :, bass.ds(b * S, S)]).then_inc(xs_ready, 1)

        @block.tensor
        def _(pe):
            for s in (p_full, kv_full, t_full, o_full, ot_full, y_full):
                pe.sem_inc(s, CREDIT)
            pe.wait_ge(w_in, NW * 16)
            with pe.Fori(0, B) as b:
                def free(j):
                    pe.wait_ge(p_read[j % 2], CREDIT + b * (JOBS // 2) + j // 2)

                pe.wait_ge(xs_ready, b + 1)
                for j in range(6):
                    free(j)
                    for x in range(1 if j < 4 else 2):
                        for k in range(KD):
                            if j < 4:
                                ins = pe.matmul(ps_p[j % 2][:, :], (wq, wk)[j // 2][:, k, (j % 2) * P:(j % 2 + 1) * P],
                                                xs[:, k, :], start=k == 0, stop=k == KD - 1)
                            else:
                                t = 2 * (j - 4) + x
                                ins = pe.matmul(ps_p[j % 2][:, x * D:(x + 1) * D], xs[:, k, t * P:(t + 1) * P],
                                                wv[:, k, :], start=k == 0, stop=k == KD - 1)
                    ins.then_inc(p_full, 1)

                def features(which, t):
                    for g in range(HG):
                        j = 6 + ((1 - which) * TPB + t) * HG + g
                        free(j)
                        pe.matmul(ps_p[j % 2][:, :], qk[:, which, g, t * P:(t + 1) * P], pm[:, :],
                                  start=True, stop=True).then_inc(p_full, 1)

                def turn(t):
                    n = b * TPB + t
                    pe.wait_ge(o_ready, CREDIT + n + 1)
                    pe.wait_ge(oT_ready, CREDIT + n)
                    for k in range(KD):
                        ins = pe.transpose(ps_ot[:, k, :], o[:, t % 2, k * P:(k + 1) * P], ident[:, :])
                    ins.then_inc(ot_full, 1)

                def result(t):
                    n = b * TPB + t
                    pe.wait_ge(oT_ready, CREDIT + n + 1)
                    pe.wait_ge(y_added, CREDIT + n)
                    for k in range(KD):
                        ins = pe.matmul(ps_y[:, :], oT[:, t % 2, k, :], wo[:, k, :], start=k == 0, stop=k == KD - 1)
                    ins.then_inc(y_full, 1)

                for x in range(2):
                    pe.wait_ge(p_read[x], CREDIT + b * (JOBS // 2) + 3)
                for t in range(TPB):
                    features(1, t)
                features(0, 0)
                pe.wait_ge(feat_ready, CREDIT + b * NFE + TPB * HG)
                pe.wait_ge(kv_ready, CREDIT + b)
                for j in range(PAIRS):
                    for t in range(TPB):
                        ins = pe.matmul(ps_kv[:, j, :], kf[:, t, j * P:(j + 1) * P],
                                        v[:, t, 2 * j:2 * j + 2, :].rearrange("p a b -> p (a b)"),
                                        start=t == 0, stop=t == TPB - 1)
                ins.then_inc(kv_full, 1)
                for t in range(TPB):
                    n = b * TPB + t
                    if t + 1 < TPB:
                        features(0, t + 1)
                    for x in range(2):
                        pe.wait_ge(feat_ready, CREDIT + b * NFE + (TPB + t) * HG + x + 1)
                        pe.wait_ge(qfT_ready, CREDIT + n * 2 + x - 1)
                        for j in range(4):
                            ins = pe.transpose(ps_t[x][:, j, :], qf[:, t % 2, (4 * x + j) * P:(4 * x + j + 1) * P],
                                               ident[:, :])
                        ins.then_inc(t_full, 1)
                    if t == 0:
                        pe.wait_ge(kv_ready, CREDIT + b + 1)
                    else:
                        turn(t - 1)
                    pe.wait_ge(o_ready, CREDIT + n)
                    for j in range(PAIRS):
                        if j % 4 == 0:
                            pe.wait_ge(qfT_ready, CREDIT + n * 2 + j // 4 + 1)
                        ins = pe.matmul(ps_o[:, j, :], qfT[:, t % 2, j, :], kv[:, j, :], start=True, stop=True)
                    ins.then_inc(o_full, 1)
                    if t:
                        result(t - 1)
                turn(TPB - 1)
                result(TPB - 1)

        @block.scalar
        def _(act):
            for s in (feat_ready, qfT_ready, oT_ready):
                act.sem_inc(s, CREDIT)
            act.wait_ge(w_in, NW * 16)
            with act.Fori(0, B) as b:
                for j in range(4):
                    act.wait_ge(p_full, CREDIT + b * JOBS + j + 1)
                    act.activation(qk[:, j // 2, j % 2, :], ps_p[j % 2][:, :], ACT.Identity,
                                   bias=cols[:, j:j + 1]).then_inc(p_read[j % 2], 1)

                def exps(which, t):
                    if which == 0:
                        act.wait_ge(t_full, CREDIT + (b * TPB + t - 1) * 2)
                    else:
                        act.wait_ge(kv_full, CREDIT + b)
                    for g in range(HG):
                        f = ((1 - which) * TPB + t) * HG + g
                        dst = qf[:, t % 2, :] if which == 0 else kf[:, t, :]
                        act.wait_ge(shift_ready, b * NFE + f + 1)
                        act.activation(dst[:, g * S:(g + 1) * S], shifted[:, g, :], ACT.Exp, scale=NORM,
                                       bias=cols[:, 4:5]).then_inc(feat_ready, 1)

                def take_turned(t):
                    n = b * TPB + t
                    act.wait_ge(ot_full, CREDIT + n + 1)
                    act.wait_ge(y_full, CREDIT + n - 1)
                    act.activation(oT[:, t % 2, :, :], ps_ot[:, :, :], ACT.Copy).then_inc(oT_ready, 1)

                for t in range(TPB):
                    exps(1, t)
                exps(0, 0)
                for t in range(TPB):
                    n = b * TPB + t
                    if t + 1 < TPB:
                        exps(0, t + 1)
                    act.wait_ge(o_full, CREDIT + n - 1)
                    for x in range(2):
                        act.wait_ge(t_full, CREDIT + n * 2 + x + 1)
                        act.activation(qfT[:, t % 2, 4 * x:4 * x + 4, :], ps_t[x][:, :, :], ACT.Copy)\
                            .then_inc(qfT_ready, 1)
                    if t:
                        take_turned(t - 1)
                take_turned(TPB - 1)

        @block.vector
        def _(dve):
            ch = Chain(dve, s_dve)
            for s in (*p_read, kv_ready, o_ready, y_added):
                dve.sem_inc(s, CREDIT)
            dve.memset(v[:, :, :, :], 1.0).then_inc(ones_set, 1)
            dve.wait_ge(ones_set, 1)
            dve.wait_ge(w_in, NW * 16)

            def add(n):
                dve.wait_ge(y_full, CREDIT + n + 1)
                dve.tensor_tensor(h[:, n, :], h[:, n, :], ps_y[:, :], ALU.add).then_inc(y_added, 1)

            with dve.Fori(0, B) as b:
                ch.restart()
                for j in (4, 5):
                    dve.wait_ge(p_full, CREDIT + b * JOBS + j + 1)
                    dve.wait_ge(kv_full, CREDIT + b)
                    for x in range(2):
                        ins = dve.tensor_tensor(v[:, 2 * (j - 4) + x, :, 0:HD],
                                                ps_p[j % 2][:, x * D:(x + 1) * D].rearrange("p (n w) -> p n w", w=HD),
                                                bv[:, :].rearrange("p (n w) -> p n w", w=HD), ALU.add)
                    ins.then_inc(p_read[j % 2], 1)

                def shift(which, t):
                    for g in range(HG):
                        f = ((1 - which) * TPB + t) * HG + g
                        j = 6 + f
                        src = ps_p[j % 2][:, :].rearrange("p (g f) -> p g f", f=NFT)
                        dve.wait_ge(p_full, CREDIT + b * JOBS + j + 1)
                        ch.link(dve.tensor_reduce(top[:, g, :], src, X, ALU.max))
                        dve.wait_ge(feat_ready, CREDIT + b * NFE + f - 1)
                        ch.link(dve.tensor_tensor(shifted[:, g, :].rearrange("p (g f) -> p g f", f=NFT), src,
                                                  top[:, g, :].unsqueeze(2).to_broadcast([P, G, NFT]),
                                                  ALU.subtract))
                        dve.sem_inc(p_read[j % 2], 1)
                        dve.sem_inc(shift_ready, 1)

                for t in range(TPB):
                    shift(1, t)
                shift(0, 0)
                dve.wait_ge(kv_full, CREDIT + b + 1)
                dve.wait_ge(o_full, CREDIT + b * TPB)
                dve.tensor_tensor(kv[:, :, :], ps_kv[:, :, :],
                                  own[:, :].unsqueeze(1).to_broadcast([P, PAIRS, W2]), ALU.mult)\
                    .then_inc(kv_ready, 1)
                for t in range(TPB):
                    n = b * TPB + t
                    if t + 1 < TPB:
                        shift(0, t + 1)
                    dve.wait_ge(o_full, CREDIT + n + 1)
                    dve.wait_ge(ot_full, CREDIT + n - 1)
                    src = ps_o[:, :, :].rearrange("p j (two w) -> p (j two) w", w=VA)
                    ch.link(dve.tensor_scalar(den[:, t % 2, :], src[:, :, HD], 1e-6, None, ALU.add))
                    ch.link(dve.reciprocal(den[:, t % 2, :], den[:, t % 2, :]))
                    dve.tensor_tensor(o[:, t % 2, :].rearrange("p (n w) -> p n w", w=HD), src[:, :, 0:HD],
                                      den[:, t % 2, :].unsqueeze(2).to_broadcast([P, NH, HD]),
                                      ALU.mult).then_inc(o_ready, 1)
                    if t:
                        add(n - 1)
                add(b * TPB + TPB - 1)


def fold_stage(nc, ident, a, w1, w2, b1, bias):
    STAGES_ = F.bit_length() - 1
    R1 = KD + 1
    with Stage(nc, "fold") as st:
        up = st.sb("up", [P, 2, 4, F // 2])
        down = st.sb("down", [P, 2, 4, F // 2])
        x = [st.sb(f"x{k}", [P, R1, F]) for k in range(2)]
        z = [st.sb(f"z{k}", [P, KD, F]) for k in range(2)]
        xt = st.sb("xt", [P, R1, F // 2])
        zt = st.sb("zt", [P, KD, F // 2])
        ub = st.sb("ub", [P, F])
        bcol = st.sb("bcol", [P, D])
        ps_t = [st.ps([P, S]) for k in range(4)]
        ps_b = st.ps([P, KF])
        in_x, in_z, in_b, zeroed, s_dve, s_pool = (st.sem(n) for n in ("in_x", "in_z", "in_b", "zeroed", "dve", "pool"))
        up_in, down_in = ([st.sem(f"{n}{k}") for k in range(2)] for n in ("up_in", "down_in"))
        up_done, down_done, t_full, x_ready, z_ready = (st.sem(n) for n in (
            "up_done", "down_done", "t_full", "x_ready", "z_ready"))
        t_read, b_full = st.sem("t_read"), st.sem("b_full")
        block = st.ctx.enter_context(nc.Block())

        @block.sync
        def _(sp):
            sp.dma_start(z[0][:, :, :], a["wconT"]).then_inc(in_z, 16)
            sp.dma_start(x[0][:, 0:KD, :], a["wexp"]).then_inc(in_x, 16)
            sp.wait_ge(zeroed, 1)
            sp.dma_start(x[0][0:1, KD, :], a["bexp"]).then_inc(in_x, 16)
            sp.dma_start(ub[0:1, :], a["upbias"]).then_inc(in_x, 16)
            sp.dma_start(bias[:, :], a["bcon"]).then_inc(in_b, 16)
            sp.dma_start(bcol[:, :], a["dbias"]).then_inc(in_b, 16)
            for s in range(STAGES_):
                if s >= 2:
                    sp.wait_ge(up_done, s - 1)
                sp.dma_start(up[:, s % 2, :, :].rearrange("p a n -> p (a n)"),
                             a["upw"][s:s + 1, :].to_broadcast([P, 2 * F])).then_inc(up_in[s % 2], 16)
                if s >= 2:
                    sp.wait_ge(down_done, s - 1)
                r = STAGES_ - 1 - s
                sp.dma_start(down[:, s % 2, :, :].rearrange("p a n -> p (a n)"),
                             a["downw"][r:r + 1, :].to_broadcast([P, 2 * F])).then_inc(down_in[s % 2], 16)

        def butterfly(eng, ch, src, dst, tmp, w, log, rows, transposed):
            n = 1 << log
            pairs = lambda v, k: v[:, :, :].rearrange("p c (b two n) -> p c b two n", two=2, n=n)[:, :, :, k, :]
            m = lambda o, i: w[:, 2 * i + o if transposed else 2 * o + i, :].rearrange(
                "p (b n) -> p b n", n=n).unsqueeze(1).to_broadcast([P, rows, F // (2 * n), n])
            t = tmp[:, :, :].rearrange("p c (b n) -> p c b n", n=n)
            for o in range(2):
                eng.tensor_tensor(pairs(dst, o), pairs(src, 0), m(o, 0), ALU.mult)
                ch.link(eng.tensor_tensor(t, pairs(src, 1), m(o, 1), ALU.mult))
                ch.link(eng.tensor_tensor(pairs(dst, o), pairs(dst, o), t, ALU.add))

        @block.vector
        def _(dve):
            ch = Chain(dve, s_dve)
            dve.memset(x[0][:, KD, :], 0.0).then_inc(zeroed, 1)
            dve.wait_ge(in_x, 48)
            for s in range(STAGES_):
                dve.wait_ge(up_in[s % 2], 16 * (s // 2 + 1))
                butterfly(dve, ch, x[s % 2], x[1 - s % 2], xt, up[:, s % 2, :, :], s, R1, False)
                dve.sem_inc(up_done, 1)
            end = x[STAGES_ % 2]
            ch.link(dve.tensor_tensor(end[0:1, KD, :], end[0:1, KD, :], ub[0:1, :], ALU.add))
            dve.sem_inc(x_ready, 1)
            dve.tensor_copy(w1[:, 0, :, :], end[:, 0:KD, :])
            dve.wait_ge(in_b, 32)
            dve.tensor_tensor(bias[:, :], bias[:, :], bcol[:, :], ALU.add)
            dve.wait_ge(b_full, 1)
            dve.tensor_copy(b1[:, 0, :], ps_b[:, :])

        @block.gpsimd
        def _(pool):
            ch = Chain(pool, s_pool)
            pool.wait_ge(in_z, 16)
            for s in range(STAGES_):
                pool.wait_ge(down_in[s % 2], 16 * (s // 2 + 1))
                butterfly(pool, ch, z[s % 2], z[1 - s % 2], zt, down[:, s % 2, :, :], STAGES_ - 1 - s, KD, True)
                pool.sem_inc(down_done, 1)
            pool.sem_inc(z_ready, 1)

        @block.tensor
        def _(pe):
            pe.wait_ge(x_ready, 1)
            for f in range(KF):
                ins = pe.transpose(ps_b[:, f:f + 1], x[STAGES_ % 2][0:1, KD, f * P:(f + 1) * P], ident[0:1, 0:1])
            ins.then_inc(b_full, 1)
            pe.wait_ge(z_ready, 1)
            for q in range(KF // 2):
                for f in (2 * q, 2 * q + 1):
                    for k in range(KD):
                        ins = pe.transpose(ps_t[q][:, (2 * (f % 2) + k) * P:(2 * (f % 2) + k + 1) * P],
                                           z[STAGES_ % 2][:, k, f * P:(f + 1) * P], ident[:, :])
                ins.then_inc(t_full, 1)

        @block.scalar
        def _(act):
            for q in range(KF // 2):
                act.wait_ge(t_full, q + 1)
                act.activation(w2[:, 0, 2 * q:2 * q + 2, :], ps_t[q][:, :].rearrange("p (f d) -> p f d", f=2),
                               ACT.Copy)


def _l0_attn(nc, a, h, xnT, ident):
    norm_stage(nc, "n1", h, xnT, ident)
    l0_attn_stage(nc, h, xnT, ident, a["wq0"], a["wk0"], a["wv0"], a["wo0"])


def _tok(nc, a, h, xnT, ident):
    token_stage(nc, h, ident, a)


def _l0_ffn(nc, a, h, xnT, ident):
    norm_stage(nc, "n2", h, xnT, ident)
    l0_ffn_stage(nc, h, xnT, ident, a)


def _l1_ffn(nc, a, h, xnT, ident):
    norm_stage(nc, "n4", h, xnT, ident)
    l1_ffn_stage(nc, h, xnT, a)


def _l1_attn(nc, a, h, xnT, ident):
    norm_stage(nc, "n3", h, xnT, ident)
    l1_attn_stage(nc, h, xnT, ident, a)


def _l2_attn(nc, a, h, xnT, ident):
    norm_stage(nc, "n5", h, xnT, ident)
    l2_attn_stage(nc, h, xnT, ident, a)


def _l3_attn(nc, a, h, xnT, ident):
    norm_stage(nc, "n7", h, xnT, ident)
    l3_attn_stage(nc, h, xnT, ident, a)


def _l2_ffn(nc, a, h, xnT, ident):
    norm_stage(nc, "n6", h, xnT, ident)

    def load(sp, e, w1, w2, b1, sem):
        if isinstance(e, int):
            s1, s2, s3 = (a[n][e, :, :] for n in ("moe_w1", "moe_w2", "moe_b1"))
        else:
            s1, s2, s3 = (a[n][bass.ds(e, 1), :, :].rearrange("o p n -> p (o n)")
                          for n in ("moe_w1", "moe_w2", "moe_b1"))
        sp.dma_start(w1.rearrange("p k n -> p (k n)"), s1).then_inc(sem, 16)
        sp.dma_start(w2.rearrange("p k n -> p (k n)"), s2).then_inc(sem, 16)
        sp.dma_start(b1, s3).then_inc(sem, 16)

    with Stage(nc, "l2f") as st:
        gates = st.sb("gates", [P, TILES, WE])
        routing_stage(nc, h, xnT, ident, a, gates)
        ffn_stage(nc, "moe", h, xnT, WE, load, gates=gates)


def _l3_ffn(nc, a, h, xnT, ident):
    norm_stage(nc, "n8", h, xnT, ident)
    with Stage(nc, "l3f") as st:
        w1 = st.sb("w1", [P, 1, KD, F])
        w2 = st.sb("w2", [P, 1, KF, D])
        b1 = st.sb("b1", [P, 1, KF])
        bias = st.sb("bias", [P, D])
        fold_stage(nc, ident, a, w1, w2, b1, bias)
        ffn_stage(nc, "out", h, xnT, 1, None, w1=w1, w2=w2, b1=b1, bias=bias[:, :])

STAGES = {"tok": _tok, "l0_attn": _l0_attn, "l0_ffn": _l0_ffn, "l1_attn": _l1_attn, "l1_ffn": _l1_ffn,
          "l2_attn": _l2_attn, "l2_ffn": _l2_ffn, "l3_attn": _l3_attn, "l3_ffn": _l3_ffn}


def program(nc, a, out):
    with Stage(nc, "all") as st:
        Stage.banks = [st.ctx.enter_context(nc.psum_tensor(f"bank{k}", [P, 512], F32)) for k in range(8)]
        h = st.sb("h", [P, TILES, D])
        xnT = st.sb("xnT", [P, KD, B * S])
        ident = st.sb("ident", [P, P])
        loaded, stored = st.sem("loaded"), st.sem("stored")
        with nc.Block() as block:
            @block.sync
            def _(sp):
                sp.dma_start(ident[:, :], a["c_ident"]).then_inc(loaded, 16)
                sp.wait_ge(loaded, 16)
        for stage in STAGES.values():
            stage(nc, a, h, xnT, ident)
        with nc.Block() as block:
            @block.sync
            def _(sp):
                sp.dma_start(out.rearrange("(t p) d -> p t d", p=P), h[:, :, :]).then_inc(stored, 16)
                sp.wait_ge(stored, 16)


def k_major(w):
    return np.ascontiguousarray(w.reshape(-1, P, w.shape[-1]).transpose(1, 0, 2))


def arrays(x):
    f = {k: np.asarray(v) for k, v in x.items()}
    r = {"c_ident": np.eye(P, dtype=np.float32)}
    r["wq0"], r["wk0"], r["wv0"] = (k_major(f[f"L0_attn_w{n}"].T) for n in "qkv")
    r["wo0"] = k_major(f["L0_attn_wo"].T)
    rows = lambda v, n=P: np.ascontiguousarray(np.broadcast_to(v, (n, v.shape[-1])))
    hours, days, mins = (f[n].reshape(1, -1) for n in ("x", "itok_BS_1_7", "itok_BS_0_1439"))
    r["idx"] = np.ascontiguousarray(np.concatenate([rows(hours, 32), rows(days, 32), rows(mins, 2), rows(days, 2)]))
    tab = np.zeros((64, P), np.float32)
    tab[0:25, 0:64], tab[32:40, 64:] = f["L0_tok_hour_tab"], f["L0_tok_wd_tab"]
    w1 = np.zeros((5, P), np.float32)
    w1[0:2, 0:64], w1[2:4, 64:] = f["L0_tok_t_w1"], f["L0_tok_d_w1"]
    w1[4, 0:64], w1[4, 64:] = f["L0_tok_t_b1"], f["L0_tok_d_b1"]
    w2 = np.zeros((P, P), np.float32)
    w2[0:64, 0:64], w2[64:, 64:] = f["L0_tok_t_w2"], f["L0_tok_d_w2"]
    r["tab"], r["tok_w1"], r["tok_w2"] = tab, w1, w2
    r["proj_w"], r["proj_b"] = k_major(f["L0_tok_proj_w"]), rows(f["L0_tok_proj_b"])
    turn = np.array([1440.0, 1440.0, 28.0, 28.0], np.float32)
    step = np.nextafter((2 * np.pi / turn).astype(np.float32), np.float32(0))
    cols = np.zeros((P, 8), np.float32)
    for k, n in enumerate(("gamma", "beta", "b2")):
        cols[0:64, k], cols[64:, k] = f[f"L0_tok_t_{n}"], f[f"L0_tok_d_{n}"]
    cols[:, 3] = np.arange(P) % 32
    cols[0:32, 4], cols[32:64, 4] = 24, 7
    cols[0:4, 5], cols[0:4, 6], cols[:, 7] = 1 / turn, -turn, LN_EPS
    r["tok_cols"] = cols
    r["c_fcols"] = np.stack([np.array([1, 1, 4, 4], np.float32), np.array([0, 360, 0, 7], np.float32), step], 1)
    r["m1"] = k_major(f["L0_ffn_m1"])
    r["m2"] = np.concatenate([f["L0_ffn_m2"].reshape(64, -1), f["L0_ffn_mb"].reshape(1, -1)])
    r["w1_0"] = k_major(f["L0_ffn_w1"].reshape(D, -1))
    r["w2_0"] = k_major(f["L0_ffn_w2"].transpose(1, 0, 2).reshape(-1, D))
    r["b2_0"] = rows(f["L0_ffn_b2"])
    r["c_rank"] = rows(np.arange(64, 0, -1)).astype(np.float32)
    w = np.stack([k_major(f[f"L1_attn_W{n}"]).reshape(P, KD, 8, P) for n in "qkgv"], 1)
    r["l1_w"] = np.ascontiguousarray(w.transpose(3, 0, 1, 2, 4)).reshape(8, P, -1)
    r["l1_wo"] = f["L1_attn_Wo"].reshape(8, P, D)
    masks = np.zeros((P, 7, P), np.float32)
    s, t = np.arange(P)[:, None], np.arange(P)[None, :]
    for k in range(7):
        masks[:, k, :] = (s >> (k + 1) == t >> (k + 1)) & (s >> k < t >> k)
    r["c_masks"] = masks
    twice = lambda w: np.concatenate([w, w], -1)
    halves = lambda w: np.concatenate([w[:, 0:8], w[:, 8:16]])
    r["win"] = k_major(twice(f["L1_ffn_Win"]))
    r["wout"] = np.concatenate([f["L1_ffn_Wout"]] * 2)
    r["bout"] = rows(f["L1_ffn_bout"])
    b2 = np.concatenate([f["L1_ffn_b2"], np.zeros(64, np.float32)])
    r["l1f_cols"] = np.concatenate([halves(f["L1_ffn_W1"]), halves(f["L1_ffn_b1"]), halves(f["L1_ffn_W2"]),
                                    twice(f["L1_ffn_bin_"])[:, None], b2[:, None]], 1)
    for n in "qkvo":
        r[f"w{n}2"] = k_major(f[f"L2_attn_W{n}"].T)
    r["c_heads"] = (np.arange(P)[:, None] // 16 == np.arange(8)[None, :]).astype(np.float32)
    r["c_future"] = np.where(np.arange(P)[None, :] > np.arange(P)[:, None], np.float32(-1e30), np.float32(0))
    w, bias = f["L3_attn_W_qkv"].T, f["L3_attn_b_qkv"]
    r["wq3"], r["wk3"], r["wv3"] = (k_major(w[:, k * D:(k + 1) * D]) for k in range(3))
    r["wo3"] = k_major(f["L3_attn_W_proj"].T)
    pm = np.zeros((8, 16, 8, 64), np.float32)
    for g in range(8):
        pm[g, :, g, :] = f["L3_attn_proj_mat"].T
    r["pm3"] = pm.reshape(P, 512)
    eps = np.full((P, 1), 1e-4, np.float32)
    r["l3a_cols"] = np.concatenate([bias[0:2 * D].reshape(4, P).T, eps], 1)
    r["bv3"], r["bo3"] = rows(bias[2 * D:]), rows(f["L3_attn_b_proj"])
    own = np.zeros((2, 64, 2, 17), np.float32)
    own[0, :, 0], own[1, :, 1] = 1, 1
    r["c_own"] = own.reshape(P, 34)
    every = lambda n: np.concatenate([f[f"L2_ffn_{n}"], f[f"L2_ffn_f{n.lower()}"][None]])
    r["wr"] = k_major(f["L2_ffn_Wr"].T)
    r["moe_w1"] = np.stack([k_major(w).reshape(P, -1) for w in every("W1")])
    r["moe_w2"] = np.stack([k_major(w).reshape(P, -1) for w in every("W2")])
    r["moe_b1"] = np.ascontiguousarray(every("b1").reshape(WE, KF, P).transpose(0, 2, 1))
    r["moe_b2"] = every("b2")
    r["c_upto"] = np.triu(np.ones((P, P), np.float32))
    r["c_rank8"] = rows(np.arange(8, 0, -1).astype(np.float32))
    r["wexp"], r["wconT"] = k_major(f["L3_ffn_W_exp"]), k_major(np.ascontiguousarray(f["L3_ffn_W_con"].T))
    r["bexp"], r["upbias"] = f["L3_ffn_b_exp"][None], f["L3_ffn_up_bias"][None]
    r["bcon"], r["dbias"] = rows(f["L3_ffn_b_con"]), rows(f["L3_ffn_down_bias"])
    for n in ("up", "down"):
        r[f"{n}w"] = np.ascontiguousarray(f[f"L3_ffn_{n}_weights"].transpose(0, 2, 3, 1)).reshape(10, -1)
    return r


def kernel(**inputs):
    import concourse.bacc as bacc
    from concourse.bass_utils import run_bass_kernel_spmd

    nc = bacc.Bacc("TRN2", target_bir_lowering=False, num_devices=1)
    data = {n: np.ascontiguousarray(v) for n, v in arrays(inputs).items()}
    a = {n: nc.dram_tensor(n, v.shape, mybir.dt.from_np(v.dtype), kind="ExternalInput").ap()
         for n, v in data.items()}
    out = nc.dram_tensor("out", (B * S, D), F32, kind="ExternalOutput").ap()
    program(nc, a, out)
    r = run_bass_kernel_spmd(nc, [data], core_ids=[0])
    return r.results[0]["out"].reshape(B, S, D)
```
